# Optimizing a Trainium2 kernel written in Bass

```python
import numpy as np
import jax
import jax.numpy as jnp

def _softmax(x, axis=-1):
    return jax.nn.softmax(x, axis=axis)

def _gelu(x):
    return jax.nn.gelu(x, approximate=True)

def _silu(x):
    return jax.nn.silu(x)

def _sigmoid(x):
    return jax.nn.sigmoid(x)

def _layernorm(x, axis=-1, eps=1e-05):
    m = jnp.mean(x, axis=axis, keepdims=True)
    v = jnp.var(x, axis=axis, keepdims=True)
    return (x - m) / jnp.sqrt(v + eps)

def _scatter_add(tgt, idx, src, axis=0):
    return tgt.at[idx].add(src)

def _segment_sum(src, seg, n):
    return jax.ops.segment_sum(src, seg, n)
kernel_name = 'mk_seq_postln_d2_jaxref_r8_988a43'

def setup_inputs(seed: int=0):
    np.random.seed(seed)
    _w = jnp.asarray

    def _L0_attn_setup():
        import jax, jax.numpy as jnp
        import numpy as np
        EMBED_DIM = 256
        NUM_HEADS = 16
        BLOCK_SIZE = 128

        def _flash_attention_v2(q, k, v, block_size, scale):
            B, H, S, D = q.shape
            nb = S // block_size
            qb = q.reshape(B, H, nb, block_size, D)
            kb = k.reshape(B, H, nb, block_size, D).transpose(2, 0, 1, 3, 4)
            vb = v.reshape(B, H, nb, block_size, D).transpose(2, 0, 1, 3, 4)
            out0 = jnp.zeros_like(qb)
            l0 = jnp.zeros((B, H, nb, block_size, 1), dtype=q.dtype)
            m0 = jnp.full((B, H, nb, block_size, 1), -jnp.inf, dtype=q.dtype)

            def step(carry, kv):
                out, l, m = carry
                k_j, v_j = kv
                s = jnp.einsum('bhnqd,bhkd->bhnqk', qb, k_j) * scale
                m_ij = jnp.max(s, axis=-1, keepdims=True)
                p = jnp.exp(s - m_ij)
                l_ij = jnp.sum(p, axis=-1, keepdims=True)
                m_new = jnp.maximum(m, m_ij)
                alpha = jnp.exp(m - m_new)
                beta = jnp.exp(m_ij - m_new)
                l_new = alpha * l + beta * l_ij
                pv = jnp.einsum('bhnqk,bhkd->bhnqd', p, v_j)
                out_new = alpha * l / l_new * out + beta * l_ij / l_new * pv
                return ((out_new, l_new, m_new), None)
            (out, _, _), _ = jax.lax.scan(step, (out0, l0, m0), (kb, vb))
            return out.reshape(B, H, S, D)
        key = jax.random.key(seed)
        k1, k2, k3 = jax.random.split(key, 3)
        B, S, E = (2, 512, EMBED_DIM)
        x = jax.random.normal(k1, (B, S, E), dtype=jnp.float32)
        w_qkv = jax.random.normal(k2, (3 * E, E), dtype=jnp.float32) * 0.02
        w_out = jax.random.normal(k3, (E, E), dtype=jnp.float32) * 0.02
        b_out = jnp.zeros((E,), dtype=jnp.float32)
        return {'x': x, 'w_qkv': w_qkv, 'w_out': w_out, 'b_out': b_out}
    _L0_attn_in = _L0_attn_setup()

    def _L0_ffn_setup():
        import jax, jax.numpy as jnp
        import numpy as np
        HIDDEN = 256
        INTER = 1024
        B, S = (4, 128)

        def _qmatmul(x, w_int8, scale):
            y = jnp.einsum('bsh,ho->bso', x, w_int8.astype(x.dtype))
            return y * scale
        key = jax.random.key(seed)
        ks = jax.random.split(key, 7)
        x = jax.random.normal(ks[0], (B, S, HIDDEN), dtype=jnp.float32)
        w_gate = jax.random.randint(ks[1], (HIDDEN, INTER), -128, 128, dtype=jnp.int32).astype(jnp.int8)
        w_up = jax.random.randint(ks[2], (HIDDEN, INTER), -128, 128, dtype=jnp.int32).astype(jnp.int8)
        w_down = jax.random.randint(ks[3], (INTER, HIDDEN), -128, 128, dtype=jnp.int32).astype(jnp.int8)
        s_gate = jax.random.uniform(ks[4], (INTER,), dtype=jnp.float32) * 0.02 + 0.001
        s_up = jax.random.uniform(ks[5], (INTER,), dtype=jnp.float32) * 0.02 + 0.001
        s_down = jax.random.uniform(ks[6], (HIDDEN,), dtype=jnp.float32) * 0.02 + 0.001
        return {'x': x, 'w_gate': w_gate, 'w_up': w_up, 'w_down': w_down, 's_gate': s_gate, 's_up': s_up, 's_down': s_down}
    _L0_ffn_in = _L0_ffn_setup()

    def _L1_attn_setup():
        import jax, jax.numpy as jnp
        import numpy as np
        HIDDEN = 256
        HEAD_DIM = 64
        N_HEADS = HIDDEN // HEAD_DIM
        ROT_DIM = HEAD_DIM // 2
        THETA = 10000.0
        SCALE_BASE = 512.0
        EPS = 1e-05
        B, S = (1, 256)

        def _rotate_half(t):
            x1 = t[..., 0::2]
            x2 = t[..., 1::2]
            return jnp.stack([-x2, x1], axis=-1).reshape(t.shape)

        def _xpos_rotary(q, k, seqlen):
            dim = ROT_DIM
            inv_freq = 1.0 / THETA ** (jnp.arange(0, dim, 2, dtype=jnp.float32) / dim)
            t = jnp.arange(seqlen, dtype=jnp.float32)
            freqs = t[:, None] * inv_freq[None, :]
            freqs = jnp.repeat(freqs, 2, axis=-1)
            base_scale = (jnp.arange(0, dim, 2, dtype=jnp.float32) + 0.4 * dim) / (1.4 * dim)
            power = (t - seqlen // 2) / SCALE_BASE
            scale = base_scale[None, :] ** power[:, None]
            scale = jnp.concatenate([scale, scale], axis=-1)
            cos, sin = (jnp.cos(freqs), jnp.sin(freqs))

            def apply(x, sc):
                xr, xp = (x[..., :dim], x[..., dim:])
                xr = xr * cos * sc + _rotate_half(xr) * sin * sc
                return jnp.concatenate([xr, xp], axis=-1)
            return (apply(q, scale), apply(k, 1.0 / scale))

        def _msr_forward(x, wqkv, wg, wo, gn_weight, gn_bias):
            b, s, _ = x.shape
            qkv = x @ wqkv.T
            qkv = qkv.reshape(b, s, N_HEADS, 3 * HEAD_DIM).transpose(0, 2, 1, 3)
            q, k, v = jnp.split(qkv, 3, axis=-1)
            q, k = _xpos_rotary(q, k, s)
            gamma = 1.0 - 2.0 ** (-5.0 - jnp.arange(N_HEADS, dtype=jnp.float32))
            idx = jnp.arange(s)
            nm = idx[:, None] - idx[None, :]
            decay = jnp.where(nm >= 0, gamma[:, None, None] ** jnp.maximum(nm, 0).astype(jnp.float32), 0.0)
            scores = jnp.einsum('bhid,bhjd->bhij', q, k) * decay
            ret = jnp.einsum('bhij,bhjd->bhid', scores, v)
            mean = ret.mean(axis=(2, 3), keepdims=True)
            var = ret.var(axis=(2, 3), keepdims=True)
            ret = (ret - mean) / jnp.sqrt(var + EPS)
            ret = ret * gn_weight[None, :, None, None] + gn_bias[None, :, None, None]
            y = ret.transpose(0, 2, 1, 3).reshape(b, s, HIDDEN)
            g = x @ wg.T
            mish = g * jnp.tanh(jax.nn.softplus(g))
            return mish * y @ wo.T
        key = jax.random.key(seed)
        ks = jax.random.split(key, 4)
        std = HIDDEN ** (-0.5)
        x = jax.random.normal(ks[0], (B, S, HIDDEN), jnp.float32)
        wqkv = jax.random.normal(ks[1], (3 * HIDDEN, HIDDEN), jnp.float32) * std
        wg = jax.random.normal(ks[2], (HIDDEN, HIDDEN), jnp.float32) * std
        wo = jax.random.normal(ks[3], (HIDDEN, HIDDEN), jnp.float32) * std
        gn_weight = jnp.ones((N_HEADS,), jnp.float32)
        gn_bias = jnp.zeros((N_HEADS,), jnp.float32)
        return {'x': x, 'wqkv': wqkv, 'wg': wg, 'wo': wo, 'gn_weight': gn_weight, 'gn_bias': gn_bias}
    _L1_attn_in = _L1_attn_setup()

    def _L1_ffn_setup():
        import jax, jax.numpy as jnp
        import numpy as np
        B, S, H = (2, 64, 256)
        E, I, K = (64, 176, 6)
        NS = 2
        SH_I = I * NS
        key = jax.random.key(seed)
        ks = jax.random.split(key, 6)
        s = 0.02
        return {'hidden_states': jax.random.normal(ks[0], (B, S, H), jnp.float32), 'gate_w': jax.random.normal(ks[1], (E, H), jnp.float32) * s, 'experts_w1': jax.random.normal(ks[2], (E, I, H), jnp.float32) * s, 'experts_w2': jax.random.normal(ks[3], (E, H, I), jnp.float32) * s, 'shared_gate_up': jax.random.normal(ks[4], (2 * SH_I, H), jnp.float32) * s, 'shared_down': jax.random.normal(ks[5], (H, SH_I), jnp.float32) * s}
    _L1_ffn_in = _L1_ffn_setup()
    _d = {'L0_attn_x': _L0_attn_in['x'], 'L0_attn_w_qkv': _L0_attn_in['w_qkv'], 'L0_attn_w_out': _L0_attn_in['w_out'], 'L0_attn_b_out': _L0_attn_in['b_out'], 'L0_ffn_w_gate': _L0_ffn_in['w_gate'], 'L0_ffn_w_up': _L0_ffn_in['w_up'], 'L0_ffn_w_down': _L0_ffn_in['w_down'], 'L0_ffn_s_gate': _L0_ffn_in['s_gate'], 'L0_ffn_s_up': _L0_ffn_in['s_up'], 'L0_ffn_s_down': _L0_ffn_in['s_down'], 'L1_attn_wqkv': _L1_attn_in['wqkv'], 'L1_attn_wg': _L1_attn_in['wg'], 'L1_attn_wo': _L1_attn_in['wo'], 'L1_attn_gn_weight': _L1_attn_in['gn_weight'], 'L1_attn_gn_bias': _L1_attn_in['gn_bias'], 'L1_ffn_gate_w': _L1_ffn_in['gate_w'], 'L1_ffn_experts_w1': _L1_ffn_in['experts_w1'], 'L1_ffn_experts_w2': _L1_ffn_in['experts_w2'], 'L1_ffn_shared_gate_up': _L1_ffn_in['shared_gate_up'], 'L1_ffn_shared_down': _L1_ffn_in['shared_down']}
    _x0 = _d['L0_attn_x']
    _d['L0_attn_x'] = jax.random.normal(jax.random.fold_in(jax.random.key(seed), 1), (2, 1024, 256), dtype=_x0.dtype)
    del _x0
    return _d

def reference(L0_attn_x, L0_attn_w_qkv, L0_attn_w_out, L0_attn_b_out, L0_ffn_w_gate, L0_ffn_w_up, L0_ffn_w_down, L0_ffn_s_gate, L0_ffn_s_up, L0_ffn_s_down, L1_attn_wqkv, L1_attn_wg, L1_attn_wo, L1_attn_gn_weight, L1_attn_gn_bias, L1_ffn_gate_w, L1_ffn_experts_w1, L1_ffn_experts_w2, L1_ffn_shared_gate_up, L1_ffn_shared_down):

    def _L0_attn_ref(x, w_qkv, w_out, b_out):
        import jax, jax.numpy as jnp
        import numpy as np
        EMBED_DIM = 256
        NUM_HEADS = 16
        BLOCK_SIZE = 128

        def _flash_attention_v2(q, k, v, block_size, scale):
            B, H, S, D = q.shape
            nb = S // block_size
            qb = q.reshape(B, H, nb, block_size, D)
            kb = k.reshape(B, H, nb, block_size, D).transpose(2, 0, 1, 3, 4)
            vb = v.reshape(B, H, nb, block_size, D).transpose(2, 0, 1, 3, 4)
            out0 = jnp.zeros_like(qb)
            l0 = jnp.zeros((B, H, nb, block_size, 1), dtype=q.dtype)
            m0 = jnp.full((B, H, nb, block_size, 1), -jnp.inf, dtype=q.dtype)

            def step(carry, kv):
                out, l, m = carry
                k_j, v_j = kv
                s = jnp.einsum('bhnqd,bhkd->bhnqk', qb, k_j) * scale
                m_ij = jnp.max(s, axis=-1, keepdims=True)
                p = jnp.exp(s - m_ij)
                l_ij = jnp.sum(p, axis=-1, keepdims=True)
                m_new = jnp.maximum(m, m_ij)
                alpha = jnp.exp(m - m_new)
                beta = jnp.exp(m_ij - m_new)
                l_new = alpha * l + beta * l_ij
                pv = jnp.einsum('bhnqk,bhkd->bhnqd', p, v_j)
                out_new = alpha * l / l_new * out + beta * l_ij / l_new * pv
                return ((out_new, l_new, m_new), None)
            (out, _, _), _ = jax.lax.scan(step, (out0, l0, m0), (kb, vb))
            return out.reshape(B, H, S, D)
        B, S, E = x.shape
        H = NUM_HEADS
        D = E // H
        scale = 1.0 / np.sqrt(D).astype(np.float32)
        qkv = (x @ w_qkv.T).reshape(B, S, 3, H, D)
        q, k, v = jnp.moveaxis(qkv, 2, 0)
        q = q.transpose(0, 2, 1, 3)
        k = k.transpose(0, 2, 1, 3)
        v = v.transpose(0, 2, 1, 3)
        out = _flash_attention_v2(q, k, v, BLOCK_SIZE, scale)
        out = out.transpose(0, 2, 1, 3).reshape(B, S, E)
        return out @ w_out.T + b_out

    def _L0_ffn_ref(x, w_gate, w_up, w_down, s_gate, s_up, s_down):
        import jax, jax.numpy as jnp
        import numpy as np
        HIDDEN = 256
        INTER = 1024
        B, S = (4, 128)

        def _qmatmul(x, w_int8, scale):
            y = jnp.einsum('bsh,ho->bso', x, w_int8.astype(x.dtype))
            return y * scale
        gate = jax.nn.silu(_qmatmul(x, w_gate, s_gate))
        up = _qmatmul(x, w_up, s_up)
        fuse = gate * up
        return _qmatmul(fuse, w_down, s_down)

    def _L1_attn_ref(x, wqkv, wg, wo, gn_weight, gn_bias):
        import jax, jax.numpy as jnp
        import numpy as np
        HIDDEN = 256
        HEAD_DIM = 64
        N_HEADS = HIDDEN // HEAD_DIM
        ROT_DIM = HEAD_DIM // 2
        THETA = 10000.0
        SCALE_BASE = 512.0
        EPS = 1e-05
        B, S = (1, 256)

        def _rotate_half(t):
            x1 = t[..., 0::2]
            x2 = t[..., 1::2]
            return jnp.stack([-x2, x1], axis=-1).reshape(t.shape)

        def _xpos_rotary(q, k, seqlen):
            dim = ROT_DIM
            inv_freq = 1.0 / THETA ** (jnp.arange(0, dim, 2, dtype=jnp.float32) / dim)
            t = jnp.arange(seqlen, dtype=jnp.float32)
            freqs = t[:, None] * inv_freq[None, :]
            freqs = jnp.repeat(freqs, 2, axis=-1)
            base_scale = (jnp.arange(0, dim, 2, dtype=jnp.float32) + 0.4 * dim) / (1.4 * dim)
            power = (t - seqlen // 2) / SCALE_BASE
            scale = base_scale[None, :] ** power[:, None]
            scale = jnp.concatenate([scale, scale], axis=-1)
            cos, sin = (jnp.cos(freqs), jnp.sin(freqs))

            def apply(x, sc):
                xr, xp = (x[..., :dim], x[..., dim:])
                xr = xr * cos * sc + _rotate_half(xr) * sin * sc
                return jnp.concatenate([xr, xp], axis=-1)
            return (apply(q, scale), apply(k, 1.0 / scale))

        def _msr_forward(x, wqkv, wg, wo, gn_weight, gn_bias):
            b, s, _ = x.shape
            qkv = x @ wqkv.T
            qkv = qkv.reshape(b, s, N_HEADS, 3 * HEAD_DIM).transpose(0, 2, 1, 3)
            q, k, v = jnp.split(qkv, 3, axis=-1)
            q, k = _xpos_rotary(q, k, s)
            gamma = 1.0 - 2.0 ** (-5.0 - jnp.arange(N_HEADS, dtype=jnp.float32))
            idx = jnp.arange(s)
            nm = idx[:, None] - idx[None, :]
            decay = jnp.where(nm >= 0, gamma[:, None, None] ** jnp.maximum(nm, 0).astype(jnp.float32), 0.0)
            scores = jnp.einsum('bhid,bhjd->bhij', q, k) * decay
            ret = jnp.einsum('bhij,bhjd->bhid', scores, v)
            mean = ret.mean(axis=(2, 3), keepdims=True)
            var = ret.var(axis=(2, 3), keepdims=True)
            ret = (ret - mean) / jnp.sqrt(var + EPS)
            ret = ret * gn_weight[None, :, None, None] + gn_bias[None, :, None, None]
            y = ret.transpose(0, 2, 1, 3).reshape(b, s, HIDDEN)
            g = x @ wg.T
            mish = g * jnp.tanh(jax.nn.softplus(g))
            return mish * y @ wo.T
        return _msr_forward(x, wqkv, wg, wo, gn_weight, gn_bias)

    def _L1_ffn_ref(hidden_states, gate_w, experts_w1, experts_w2, shared_gate_up, shared_down):
        import jax, jax.numpy as jnp
        import numpy as np
        B, S, H = (2, 64, 256)
        E, I, K = (64, 176, 6)
        NS = 2
        SH_I = I * NS
        orig_shape = hidden_states.shape
        x = hidden_states.reshape(-1, orig_shape[-1])
        router_logits = x @ gate_w.T
        probs = jax.nn.softmax(router_logits, axis=-1)
        topk_w, topk_idx = jax.lax.top_k(probs, K)
        topk_w = topk_w / jnp.sum(topk_w, axis=-1, keepdims=True)
        combine = jnp.sum(jax.nn.one_hot(topk_idx, E, dtype=x.dtype) * topk_w[..., None], axis=1)
        h = jax.nn.silu(jnp.einsum('th,eih->tei', x, experts_w1))
        y = jnp.einsum('tei,ehi->teh', h, experts_w2)
        routed_out = jnp.einsum('teh,te->th', y, combine)
        gu = x @ shared_gate_up.T
        g, u = jnp.split(gu, 2, axis=-1)
        shared_out = jax.nn.silu(g) * u @ shared_down.T
        return (routed_out + shared_out).reshape(orig_shape)
    x = L0_attn_x
    x = _layernorm(x + _L0_attn_ref(x, L0_attn_w_qkv, L0_attn_w_out, L0_attn_b_out), axis=-1)
    x = _layernorm(x + _L0_ffn_ref(x, L0_ffn_w_gate, L0_ffn_w_up, L0_ffn_w_down, L0_ffn_s_gate, L0_ffn_s_up, L0_ffn_s_down), axis=-1)
    x = _layernorm(x + _L1_attn_ref(x, L1_attn_wqkv, L1_attn_wg, L1_attn_wo, L1_attn_gn_weight, L1_attn_gn_bias), axis=-1)
    x = _layernorm(x + _L1_ffn_ref(x, L1_ffn_gate_w, L1_ffn_experts_w1, L1_ffn_experts_w2, L1_ffn_shared_gate_up, L1_ffn_shared_down), axis=-1)
    return x

_drawn_inputs = setup_inputs


def setup_inputs(seed=0):
    import zlib

    import numpy as np

    out = dict(_drawn_inputs(seed))
    spreads = {'L0_attn_b_out': (0.0, 0.1),
     'L1_attn_gn_weight': (1.0, 0.2),
     'L1_attn_gn_bias': (0.0, 0.1)}
    factors = {'L1_ffn_gate_w': 3.282,
     'L1_ffn_experts_w1': 3.172,
     'L1_ffn_experts_w2': 3.139,
     'L1_ffn_shared_gate_up': 2.844,
     'L1_ffn_shared_down': 2.852}
    for name, (base, spread) in spreads.items():
        noise = np.random.default_rng([zlib.crc32(name.encode()), seed]).standard_normal(out[name].shape)
        drawn = base * np.exp(spread * noise) if base else spread * noise
        out[name] = jnp.asarray(drawn.astype(out[name].dtype))
    for name, factor in factors.items():
        out[name] = (out[name] * factor).astype(out[name].dtype)
    return out
```

```python
from contextlib import ExitStack

import concourse.bass as bass
from concourse import mybir

F32 = mybir.dt.float32
BF16 = mybir.dt.bfloat16
I8 = mybir.dt.int8
I32 = mybir.dt.int32
U32 = mybir.dt.uint32
ALU = mybir.AluOpType
ACT = mybir.ActivationFunctionType
AX = mybir.AxisListType

P = 128
BATCH, SEQ, E = 2, 1024, 256
TOK = BATCH * SEQ
KT = E // P
NT = TOK // P
CH = 512
NCH = TOK // CH
EPS = 1e-5

H0, D0 = 16, 16
G0 = 4
GROUPS = BATCH * H0 // G0
KTS = SEQ // P
QC = SEQ // CH
PARTS = 3
PAIRS = ((0, 0), (0, 1), (1, 0), (1, 1), (0, 2), (2, 0))
STACK = len(PAIRS) * D0
ROWS = STACK + PARTS
SCALE0 = float(D0) ** -0.5


def scope(nc, ctx, tag):
    made = []

    def sb(name, shape, dt=F32):
        return ctx.enter_context(nc.sbuf_tensor(f"{tag}_{name}", shape, dt))

    def ps(name, shape=(P, CH), dt=F32):
        return ctx.enter_context(nc.psum_tensor(f"{tag}_{name}", list(shape), dt))

    def sem(name):
        made.append(nc.alloc_semaphore(f"{tag}_{name}"))
        return made[-1]

    def clear():
        if made:
            nc.clear_and_free_semaphores(made)
            nc.all_engine_barrier()

    ctx.callback(clear)
    return sb, ps, sem


def project_qkv(nc, a, keep):
    with ExitStack() as ctx:
        sb, ps, sem = scope(nc, ctx, "proj")
        w_qk = sb("w_qk", [P, KT, 2 * E])
        w_v = sb("w_v", [P, KT, E])
        x_t = keep["x_t"]
        SLOTS = 4
        parts = sb("parts", [P, SLOTS, PARTS, CH], BF16)
        rest = sb("rest", [P, 2, CH])
        qk_ps = [ps(f"qk{i}") for i in range(3)]
        v_ps = [ps(f"v{i}") for i in range(2)]
        loaded = [sem(f"loaded{c}") for c in range(NCH)]
        weights = sem("weights")
        v_weights = sem("v_weights")
        projected, high_done, rest_done, mid_done, low_done = (sem(n) for n in (
            "projected", "high_done", "rest_done", "mid_done", "low_done"))
        saved = [sem(f"saved{i}") for i in range(SLOTS)]
        v_done, v_kept = sem("v_done"), sem("v_kept")
        cleared = sem("cleared")
        v_all, ident, ident_bf = keep["v_all"], keep["ident"], keep["ident_bf"]
        x, bias = keep["x"], sb("bias", [P, E])
        x_in, biased = sem("x_in"), sem("biased")
        blocks = [(c, m) for c in range(NCH) for m in range(4)]
        writes = {n: 0 for n in range(len(blocks))}
        done_by = []
        count = [0] * SLOTS
        for n, (c, m) in enumerate(blocks):
            k = 3 if (c < QC and m % 2 == 0) else 2
            count[n % SLOTS] += 16 * k
            done_by.append(count[n % SLOTS])

        block = ctx.enter_context(nc.Block())

        @block.sync
        def _(sp):
            sp.dma_start(w_qk[:], a["w_qk"].rearrange("(k p) n -> p k n", p=P)).then_inc(weights, 16)
            for c in range(NCH):
                sp.dma_start(x_t[:, :, c * CH:(c + 1) * CH],
                             a["x_t"].rearrange("(k p) n -> p k n", p=P)[:, :, c * CH:(c + 1) * CH]
                             ).then_inc(loaded[c], 16)
            sp.dma_start(x[:], a["x"].rearrange("(t p) n -> p t n", p=P)).then_inc(x_in, 16)
            sp.dma_start(bias[:], a["b_out"].partition_broadcast(P)).then_inc(x_in, 16)
            for n, (c, m) in enumerate(blocks):
                sp.wait_ge(low_done, n + 1)
                qk, half, b, cc = m // 2, m % 2, c // QC, c % QC
                for p in range(2):
                    group = 2 * (2 * b + half) + p
                    for g in ([group, GROUPS] if group == 0 else [group]):
                        sp.dma_start(a["parts"][g, qk, :, :, cc * CH:(cc + 1) * CH].rearrange("a r t -> r a t"),
                                     parts[64 * p:64 * p + 64, n % SLOTS]).then_inc(saved[n % SLOTS], 16)
            for slot in range(SLOTS):
                sp.wait_ge(saved[slot], count[slot])

        @block.gpsimd
        def _(pool):
            done = 0

            def ordered(instruction):
                nonlocal done
                instruction.then_inc(cleared, 1)
                done += 1
                pool.wait_ge(cleared, done)

            for m in (ident, ident_bf):
                ordered(pool.memset(m[:], 0.0))
                ordered(pool.affine_select(out=m[:], in_=m[:], compare_op=ALU.not_equal, fill=1.0,
                                           base=0, pattern=[[-1, P]], channel_multiplier=1))
            ordered(pool.memset(v_all[:, 2 * BATCH], 0.0))
            ordered(pool.memset(keep["neg_half"][:], -0.5))
            for buf in range(2):
                ordered(pool.memset(keep["v_st"][buf][:], 1.0))
                rows = keep["k_st"][buf][STACK:P].rearrange("r h (j k) -> r h j k", k=P)
                ordered(pool.memset(rows, 0.0))
                for part in range(PARTS):
                    ordered(pool.affine_select(out=rows, in_=rows, compare_op=ALU.not_equal, fill=1.0,
                                               base=-KTS * part, pattern=[[0, G0], [-1, KTS], [0, P]],
                                               channel_multiplier=1))
            pool.wait_ge(x_in, 32)
            for t in range(NT):
                pool.tensor_tensor(x[:, t], x[:, t], bias[:], ALU.add).then_inc(biased, 1)

        @block.tensor
        def _(pe):
            pe.wait_ge(weights, 16)
            for n, (c, m) in enumerate(blocks):
                if m == 0:
                    pe.wait_ge(loaded[c], 16)
                if n >= 3:
                    pe.wait_ge(rest_done, n - 2)
                for k in range(KT):
                    mm = pe.matmul(qk_ps[n % 3][:], w_qk[:, k, m * P:(m + 1) * P],
                                   x_t[:, k, c * CH:(c + 1) * CH], start=(k == 0), stop=(k == KT - 1))
                mm.then_inc(projected, 1)
            pe.wait_ge(v_weights, 16)
            for t in range(NT):
                if t >= 2:
                    pe.wait_ge(v_kept, t - 1)
                for k in range(KT):
                    mm = pe.matmul(v_ps[t % 2][:, 0:E], x_t[:, k, t * P:(t + 1) * P], w_v[:, k, :],
                                   start=(k == 0), stop=(k == KT - 1))
                mm.then_inc(v_done, 1)

        @block.scalar
        def _(act):
            act.dma_start(w_v[:], a["w_v"].rearrange("(k p) n -> p k n", p=P)).then_inc(v_weights, 16)
            for n in range(len(blocks)):
                act.wait_ge(projected, n + 1)
                if n >= SLOTS:
                    act.wait_ge(saved[n % SLOTS], done_by[n - SLOTS])
                act.activation(parts[:, n % SLOTS, 0], qk_ps[n % 3][:], ACT.Copy).then_inc(high_done, 1)
            for t in range(NT):
                act.wait_ge(v_done, t + 1)
                b, kt = t // KTS, t % KTS
                act.activation(v_all[:, 2 * b:2 * b + 2, kt, :],
                               v_ps[t % 2][:, 0:E].rearrange("p (j n) -> p j n", j=2), ACT.Copy).then_inc(v_kept, 1)

        @block.vector
        def _(dve):
            for n in range(len(blocks)):
                dve.wait_ge(high_done, n + 1)
                dve.tensor_tensor(rest[:, n % 2], qk_ps[n % 3][:], parts[:, n % SLOTS, 0],
                                  ALU.subtract).then_inc(rest_done, 1)
                dve.wait_ge(rest_done, n + 1)
                dve.tensor_copy(parts[:, n % SLOTS, 1], rest[:, n % 2]).then_inc(mid_done, 1)
                dve.wait_ge(mid_done, n + 1)
                dve.tensor_tensor(parts[:, n % SLOTS, 2], rest[:, n % 2], parts[:, n % SLOTS, 1],
                                  ALU.subtract).then_inc(low_done, 1)


def attention(nc, a, keep):
    with ExitStack() as ctx:
        sb, ps, sem = scope(nc, ctx, "attn")
        v_all, ident, ident_bf, o_tok = keep["v_all"], keep["ident"], keep["ident_bf"], keep["o_tok"]
        q_st, k_st, v_st = keep["q_st"], keep["k_st"], keep["v_st"]
        QT = CH // P
        NB = G0 * QT
        probs = [sb(f"probs{i}", [P, G0, CH]) for i in range(2)]
        pv_sb = [sb(f"pv_sb{i}", [P, CH]) for i in range(2)]
        neg = sb("neg", [P, NB, KTS])
        neg_rest = sb("neg_rest", [P, NB, KTS])
        neg_least = sb("neg_least", [P, NB])
        neg_parts = sb("neg_parts", [P, NB, 32], BF16)
        gap = sb("gap", [P, NB, KTS])
        wj = [sb(f"wj{i}", [P, NB, KTS]) for i in range(2)]
        pv_t = [sb(f"pv_t{i}", [P, KTS, NB, D0 + 1]) for i in range(2)]
        coef = [sb(f"coef{i}", [P, NB, KTS]) for i in range(2)]
        total = sb("total", [P, NB])
        prod = sb("prod", [P, KTS, NB, D0])
        st_ps = [ps(f"st{h}") for h in range(G0)]
        mx_ps = [ps(f"mx{i}") for i in range(2)]
        o_ps = ps("o")
        turn_ps = ps("turn")

        stack = [sem(f"stack{i}") for i in range(2)]
        v_staged = sem("v_staged")
        scored, maxed = sem("scored"), sem("maxed")
        neg_chain, neg_split = sem("neg_chain"), sem("neg_split")
        neg_turned, neg_kept = sem("neg_turned"), sem("neg_kept")
        gap_in, wj_in = sem("gap_in"), sem("wj_in")
        st_made, exp_done, pv_done = sem("st_made"), sem("exp_done"), sem("pv_done")
        pv_copied, pv_turned, pv_kept = sem("pv_copied"), sem("pv_turned"), sem("pv_kept")
        coef_chain, coef_in, combine_chain, combined = (sem(n) for n in (
            "coef_chain", "coef_in", "combine_chain", "combined"))
        padded = sem("padded")

        UNITS = 2 * QC
        STEPS = UNITS * KTS
        SM = NB * 2
        TURNS = GROUPS // 2
        LOADS = (1 + QC) * len(PAIRS)
        DEAL = [5, 5, 5, 5, 4, 4, 4, 0]
        BEFORE = 2

        block = ctx.enter_context(nc.Block())

        @block.sync
        def _(sp):
            def load_stack(buf, g):
                for j, (qp, kp) in enumerate(PAIRS):
                    rows = slice(D0 * j, D0 * j + D0)
                    q_part = a["parts"][g, 0, qp].rearrange("(h d) t -> d h t", d=D0)
                    k_part = a["parts"][g, 1, kp].rearrange("(h d) t -> d h t", d=D0)
                    sp.dma_start(k_st[buf][rows], k_part).then_inc(stack[buf], 16)
                    for c in range(QC):
                        sp.dma_start(q_st[buf][rows, c], q_part[:, :, c * CH:(c + 1) * CH]).then_inc(stack[buf], 16)

            load_stack(0, 0)
            with sp.Fori(0, TURNS) as i:
                sp.wait_ge(st_made, i * (STEPS * G0))
                load_stack(1, 2 * i + 1)
                sp.wait_ge(st_made, i * (STEPS * G0) + STEPS * G0 // 2)
                load_stack(0, 2 * i + 2)
            sp.wait_ge(stack[0], 16 * LOADS * (TURNS + 1))

        @block.gpsimd
        def _(pool):
            def stage_v(buf, i):
                pool.tensor_copy(v_st[buf][:, :, :, 0:D0],
                                 v_all[:, i, :, 64 * buf:64 * buf + 64].rearrange("p k (h d) -> p k h d", d=D0)
                                 ).then_inc(v_staged, 1)

            pool.memset(prod[:], 0.0).then_inc(combined, 1)
            pool.wait_ge(combined, 1)
            stage_v(0, 0)
            with pool.Fori(0, TURNS) as i:
                def combine(w):
                    u = i * UNITS + w
                    pool.wait_ge(coef_in, u + 1)
                    pool.tensor_tensor(prod[:], pv_t[w % 2][:, :, :, 0:D0],
                                       coef[w % 2][:].rearrange("p n k -> p k n").unsqueeze(3)
                                       .to_broadcast([P, KTS, NB, D0]), ALU.mult).then_inc(combine_chain, 1)
                    pool.wait_ge(combine_chain, i * (3 * UNITS) + 3 * w + 1)
                    pool.tensor_tensor(prod[:, 0:4], prod[:, 0:4], prod[:, 4:8], ALU.add).then_inc(combine_chain, 1)
                    pool.wait_ge(combine_chain, i * (3 * UNITS) + 3 * w + 2)
                    pool.tensor_tensor(prod[:, 0:2], prod[:, 0:2], prod[:, 2:4], ALU.add).then_inc(combine_chain, 1)
                    pool.wait_ge(combine_chain, i * (3 * UNITS) + 3 * w + 3)
                    c, p = w % 2, w // 2
                    out = o_tok[:, i, c * QT:(c + 1) * QT, 64 * p:64 * p + 64].rearrange("p q (h d) -> p h q d", d=D0)
                    pool.tensor_tensor(out, prod[:, 0].rearrange("p (h q) d -> p h q d", h=G0),
                                       prod[:, 1].rearrange("p (h q) d -> p h q d", h=G0),
                                       ALU.add).then_inc(combined, 1)
                    pool.wait_ge(combined, u + 2)

                pool.wait_ge(pv_done, i * STEPS)
                stage_v(1, i)
                combine(0)
                combine(1)
                pool.wait_ge(pv_done, i * STEPS + STEPS // 2)
                stage_v(0, i + 1)
                combine(2)
                combine(3)

        @block.tensor
        def _(pe):
            def score_rows(buf, c, n):
                h, qt, half = n // (2 * QT), n // 2 % QT, n % 2
                pe.matmul(mx_ps[n % 2][:], q_st[buf][0:STACK, c, h, qt * P:(qt + 1) * P],
                          k_st[buf][0:STACK, h, half * CH:(half + 1) * CH],
                          start=True, stop=True).then_inc(scored, 1)

            def turn_neg(unit, kept):
                pe.wait_ge(neg_split, unit + 1)
                pe.wait_ge(pv_kept, kept)
                for r in range(2):
                    if r:
                        pe.wait_ge(neg_kept, unit * 2 + 1)
                    for n in range(NB // 2):
                        mm = pe.transpose(turn_ps[:].bitcast(BF16)[96:P, n * P:(n + 1) * P],
                                          neg_parts[:, r * (NB // 2) + n], ident_bf[:])
                    mm.then_inc(neg_turned, 1)

            pe.wait_ge(stack[0], 16 * LOADS)
            for n in range(SM):
                if n >= 2:
                    pe.wait_ge(maxed, n - 1)
                score_rows(0, 0, n)
            turn_neg(0, 0)
            with pe.Fori(0, TURNS) as i:
                def score_next(w, n):
                    pe.wait_ge(maxed, i * (UNITS * SM) + (SM * (w + 1) + n - 1))
                    score_rows(((w + 1) // 2) % 2, (w + 1) % 2, n)

                def pv(step):
                    w, kt = step // KTS, step % KTS
                    pe.wait_ge(pv_copied, i * STEPS + step)
                    if kt == 0 and w % 2 == 0:
                        pe.wait_ge(v_staged, 2 * i + (w // 2 + 1))
                    for h in range(G0):
                        pe.wait_ge(exp_done, i * (STEPS * G0) + (step * G0 + h + 1))
                        mm = pe.matmul(o_ps[32 * h:32 * h + 32, :], v_st[w // 2][:, kt, h], probs[step % 2][:, h],
                                       start=True, stop=True)
                    mm.then_inc(pv_done, 1)

                def turn_pv(step):
                    pe.wait_ge(pv_copied, i * STEPS + (step + 1))
                    pe.wait_ge(pv_kept, i * STEPS + step)
                    for qt in range(QT):
                        mm = pe.transpose(turn_ps[:, qt * P:(qt + 1) * P], pv_sb[step % 2][:, qt * P:(qt + 1) * P],
                                          ident[:])
                    mm.then_inc(pv_turned, 1)

                for w in range(UNITS):
                    buf, c = w // 2, w % 2
                    nbuf = ((w + 1) // 2) % 2
                    pe.wait_ge(neg_kept, i * (2 * UNITS) + 2 * (w + 1))
                    if w % 2 == 1:
                        pe.wait_ge(stack[nbuf], i * (16 * LOADS) + 16 * LOADS * (1 if nbuf else 2))
                    n = 0
                    for kt in range(KTS):
                        step = w * KTS + kt
                        todo = DEAL[kt]
                        for h in range(G0):
                            pe.wait_ge(exp_done, i * (STEPS * G0) + ((step - 1) * G0 + h + 1 if step else 0))
                            pe.matmul(st_ps[h][:], k_st[buf][:, h, kt * P:(kt + 1) * P], q_st[buf][:, c, h],
                                      start=True, stop=True).then_inc(st_made, 1)
                            if h % 2 == 1 and todo > max(0, DEAL[kt] - BEFORE):
                                score_next(w, n)
                                n, todo = n + 1, todo - 1
                        if step >= 1:
                            pv(step - 1)
                        if step >= 2:
                            turn_pv(step - 2)
                        while todo > 0:
                            score_next(w, n)
                            n, todo = n + 1, todo - 1
                    if w < UNITS - 1:
                        turn_neg(i * UNITS + w + 1, i * STEPS + ((w + 1) * KTS - 2))
                pv(STEPS - 1)
                turn_pv(STEPS - 2)
                turn_pv(STEPS - 1)
                turn_neg(i * UNITS + UNITS, i * STEPS + STEPS)

        @block.scalar
        def _(act):
            def copy_pv(i, step):
                act.wait_ge(pv_done, i * STEPS + (step + 1))
                act.wait_ge(pv_turned, i * STEPS + max(0, step - 1))
                act.activation(pv_sb[step % 2][:], o_ps[:], ACT.Copy).then_inc(pv_copied, 1)

            act.wait_ge(gap_in, 1)
            act.activation(wj[0][:], gap[:], ACT.Exp, scale=SCALE0).then_inc(wj_in, 1)
            with act.Fori(0, TURNS) as i:
                for w in range(UNITS):
                    for kt in range(KTS):
                        step = w * KTS + kt
                        act.wait_ge(pv_done, i * STEPS + max(0, step - 1))
                        for h in range(G0):
                            act.wait_ge(st_made, i * (STEPS * G0) + (step * G0 + h + 1))
                            act.activation(probs[step % 2][:, h], st_ps[h][:], ACT.Exp,
                                           scale=SCALE0).then_inc(exp_done, 1)
                        if step >= 1:
                            copy_pv(i, step - 1)
                    if w < UNITS - 1:
                        act.wait_ge(gap_in, i * UNITS + (w + 2))
                        act.wait_ge(combined, i * UNITS + (w + 1))
                        act.activation(wj[(w + 1) % 2][:], gap[:], ACT.Exp, scale=SCALE0).then_inc(wj_in, 1)
                copy_pv(i, STEPS - 1)
                act.wait_ge(gap_in, i * UNITS + (UNITS + 1))
                act.wait_ge(combined, i * UNITS + UNITS)
                act.activation(wj[0][:], gap[:], ACT.Exp, scale=SCALE0).then_inc(wj_in, 1)

        @block.vector
        def _(dve):
            def reduce(n, made):
                dve.wait_ge(scored, made)
                dve.tensor_reduce(neg[:, n // 2, n % 2 * QT:n % 2 * QT + QT],
                                  mx_ps[n % 2][:].rearrange("p (j k) -> p j k", k=P), AX.X,
                                  ALU.max, negate=True).then_inc(maxed, 1)

            def split_neg(unit):
                part = [neg_parts[:, :, j * KTS:(j + 1) * KTS] for j in range(PARTS)]
                dve.wait_ge(maxed, unit * SM + SM)
                dve.wait_ge(wj_in, unit)
                dve.tensor_copy(part[0], neg[:]).then_inc(neg_chain, 1)
                dve.tensor_reduce(neg_least[:], neg[:], AX.X, ALU.min).then_inc(neg_chain, 1)
                dve.wait_ge(neg_chain, unit * 4 + 1)
                dve.tensor_tensor(neg_rest[:], neg[:], part[0], ALU.subtract).then_inc(neg_chain, 1)
                dve.wait_ge(neg_chain, unit * 4 + 3)
                dve.tensor_copy(part[1], neg_rest[:]).then_inc(neg_chain, 1)
                dve.wait_ge(neg_chain, unit * 4 + 4)
                dve.tensor_tensor(part[2], neg_rest[:], part[1], ALU.subtract).then_inc(neg_split, 1)
                dve.tensor_tensor(gap[:], neg_least[:].unsqueeze(2).to_broadcast([P, NB, KTS]), neg[:],
                                  ALU.subtract).then_inc(gap_in, 1)

            def keep_neg(unit, buf, c):
                for r in range(2):
                    dve.wait_ge(neg_turned, unit * 2 + r + 1)
                    dve.tensor_copy(q_st[buf][96:P, c, 2 * r:2 * r + 2],
                                    turn_ps[:].bitcast(BF16)[96:P, :].rearrange("p (h t) -> p h t", h=2)
                                    ).then_inc(neg_kept, 1)

            def keep_pv(i, step):
                w, kt = step // KTS, step % KTS
                if kt == 0:
                    dve.wait_ge(combined, i * UNITS + w)
                dve.wait_ge(pv_turned, i * STEPS + (step + 1))
                dve.tensor_copy(pv_t[w % 2][:, kt].rearrange("p (h q) d -> p q h d", h=G0),
                                turn_ps[:].rearrange("p (q h d) -> p q h d", q=QT, h=G0)[:, :, :, 0:D0 + 1]
                                ).then_inc(pv_kept, 1)

            def coefficients(i, w):
                u = i * UNITS + w
                c0 = i * (3 * UNITS) + 3 * w
                dve.wait_ge(pv_kept, i * STEPS + (w + 1) * KTS)
                dve.wait_ge(wj_in, u + 1)
                dve.tensor_tensor(coef[w % 2][:], wj[w % 2][:], pv_t[w % 2][:, :, :, D0].rearrange("p k n -> p n k"),
                                  ALU.mult).then_inc(coef_chain, 1)
                dve.wait_ge(coef_chain, c0 + 1)
                dve.tensor_reduce(total[:], coef[w % 2][:], AX.X, ALU.add).then_inc(coef_chain, 1)
                dve.wait_ge(coef_chain, c0 + 2)
                dve.reciprocal(total[:], total[:]).then_inc(coef_chain, 1)
                dve.wait_ge(coef_chain, c0 + 3)
                dve.tensor_tensor(coef[w % 2][:], coef[w % 2][:], total[:].unsqueeze(2).to_broadcast([P, NB, KTS]),
                                  ALU.mult).then_inc(coef_in, 1)

            dve.memset(neg_parts[:], 0.0).then_inc(padded, 1)
            dve.wait_ge(padded, 1)
            for n in range(SM):
                reduce(n, n + 1)
            split_neg(0)
            keep_neg(0, 0, 0)
            with dve.Fori(0, TURNS) as i:
                for w in range(UNITS):
                    n = 0
                    for kt in range(KTS):
                        step = w * KTS + kt
                        todo = DEAL[kt]
                        for _ in range(min(BEFORE, todo)):
                            reduce(n, i * (UNITS * SM) + (SM * (w + 1) + n + 1))
                            n, todo = n + 1, todo - 1
                        if step >= 2:
                            keep_pv(i, step - 2)
                            if step % KTS == 1:
                                coefficients(i, w - 1)
                        for _ in range(todo):
                            reduce(n, i * (UNITS * SM) + (SM * (w + 1) + n + 1))
                            n += 1
                        if n == SM and DEAL[kt] and w < UNITS:
                            split_neg(i * UNITS + w + 1)
                    if w < UNITS - 1:
                        keep_neg(i * UNITS + w + 1, ((w + 1) // 2) % 2, (w + 1) % 2)
                keep_pv(i, STEPS - 2)
                keep_pv(i, STEPS - 1)
                coefficients(i, UNITS - 1)
                keep_neg(i * UNITS + UNITS, 0, 0)


LAG = 1
TC = CH // P


def norm_parts(makers, keep, turn=True):
    sb, ps, sem = makers
    norm = dict(x=keep["x"], x_t=keep["x_t"], ident=keep["ident"], half=keep["neg_half"],
                turn_ps=[ps(f"turn{k}") for k in range(KT)] if turn else None,
                stats=sb("ln_stats", [P, NT, 6]), mv=sb("ln_mv", [P, NT, 2]),
                var=sb("ln_var", [P, NT]), rstd=sb("ln_rstd", [P, NT]))
    for name in ("summed", "stat", "aggr", "var_in", "rstd_in", "normed", "turned", "kept"):
        norm[name] = sem(name)
    return norm


def norm_add(dve, norm, t, y):
    x = norm["x"]
    return dve.tensor_tensor(x[:, t], y, x[:, t], ALU.add).then_inc(norm["summed"], 1)


def norm_measure(dve, norm, c):
    stats, mv = norm["stats"], norm["mv"]
    for t in range(c * TC, (c + 1) * TC):
        dve.wait_ge(norm["summed"], t + 1)
        dve.bn_stats(stats[:, t], norm["x"][:, t]).then_inc(norm["stat"], 1)
    for t in range(c * TC, (c + 1) * TC):
        dve.wait_ge(norm["stat"], t + 1)
        dve.bn_aggr(mv[:, t], stats[:, t]).then_inc(norm["aggr"], 1)
    dve.wait_ge(norm["aggr"], (c + 1) * TC)
    dve.tensor_scalar(norm["var"][:, c * TC:(c + 1) * TC], mv[:, c * TC:(c + 1) * TC, 1], EPS, None,
                      ALU.add).then_inc(norm["var_in"], 1)


def norm_root(pool, norm, c):
    pool.wait_ge(norm["var_in"], c + 1)
    pool.tensor_tensor(norm["rstd"][:, c * TC:(c + 1) * TC], norm["var"][:, c * TC:(c + 1) * TC],
                       norm["half"][:, 0:TC], ALU.pow).then_inc(norm["rstd_in"], 1)


def norm_scale(dve, norm, c):
    x, mv, rstd = norm["x"], norm["mv"], norm["rstd"]
    dve.wait_ge(norm["rstd_in"], c + 1)
    for t in range(c * TC, (c + 1) * TC):
        dve.tensor_scalar(x[:, t], x[:, t], mv[:, t, 0:1], rstd[:, t:t + 1],
                          ALU.subtract, ALU.mult).then_inc(norm["normed"], 1)


def norm_turn(pe, norm, c):
    if c:
        pe.wait_ge(norm["kept"], KT * c)
    for t in range(TC):
        pe.wait_ge(norm["normed"], c * TC + t + 1)
        for k in range(KT):
            mm = pe.transpose(norm["turn_ps"][k][:, t * P:(t + 1) * P],
                              norm["x"][:, c * TC + t, k * P:(k + 1) * P], norm["ident"][:])
    mm.then_inc(norm["turned"], 1)


def norm_keep(act, norm, c):
    act.wait_ge(norm["turned"], c + 1)
    for k in range(KT):
        act.activation(norm["x_t"][:, k, c * CH:(c + 1) * CH], norm["turn_ps"][k][:],
                       ACT.Copy).then_inc(norm["kept"], 1)


def project_out(nc, a, keep):
    with ExitStack() as ctx:
        sb, ps, sem = scope(nc, ctx, "out0")
        o_tok = keep["o_tok"]
        w = sb("w", [P, KT, E])
        o_t = [sb(f"o_t{i}", [P, KT, P]) for i in range(2)]
        y_ps = [ps(f"y{i}") for i in range(2)]
        o_ps = [ps(f"o{i}") for i in range(2)]
        weights, turned, turned_in, made = (sem(n) for n in ("weights", "o_turned", "o_turned_in", "made"))
        norm = norm_parts((sb, ps, sem), keep)
        block = ctx.enter_context(nc.Block())

        @block.sync
        def _(sp):
            sp.dma_start(w[:], a["w_out"].rearrange("(k p) n -> p k n", p=P)).then_inc(weights, 16)

        @block.vector
        def _(dve):
            for c in range(NCH + LAG):
                if c < NCH:
                    for t in range(c * TC, (c + 1) * TC):
                        dve.wait_ge(made, t + 1)
                        norm_add(dve, norm, t, y_ps[t % 2][:, 0:E])
                    norm_measure(dve, norm, c)
                    norm_scale(dve, norm, c)

        @block.gpsimd
        def _(pool):
            for c in range(NCH):
                norm_root(pool, norm, c)

        @block.tensor
        def _(pe):
            def turn(t):
                b, tt = t // KTS, t % KTS
                if t >= 2:
                    pe.wait_ge(turned_in, t - 1)
                for k in range(KT):
                    mm = pe.transpose(o_ps[t % 2][:, k * P:(k + 1) * P], o_tok[:, 2 * b + k, tt], keep["ident"][:])
                mm.then_inc(turned, 1)

            turn(0)
            pe.wait_ge(weights, 16)
            for c in range(NCH + LAG):
                if c < NCH:
                    for t in range(c * TC, (c + 1) * TC):
                        if t + 1 < NT:
                            turn(t + 1)
                        pe.wait_ge(turned_in, t + 1)
                        if t >= 2:
                            pe.wait_ge(norm["summed"], t - 1)
                        for k in range(KT):
                            mm = pe.matmul(y_ps[t % 2][:, 0:E], o_t[t % 2][:, k], w[:, k],
                                           start=(k == 0), stop=(k == KT - 1))
                        mm.then_inc(made, 1)
                if c >= LAG:
                    norm_turn(pe, norm, c - LAG)

        @block.scalar
        def _(act):
            for c in range(NCH + LAG):
                if c < NCH:
                    for t in range(c * TC, (c + 1) * TC):
                        act.wait_ge(turned, t + 1)
                        if t >= 2:
                            act.wait_ge(made, t - 1)
                        act.activation(o_t[t % 2][:], o_ps[t % 2][:, 0:KT * P].rearrange("p (k t) -> p k t", k=KT),
                                       ACT.Copy).then_inc(turned_in, 1)
                if c >= LAG:
                    norm_keep(act, norm, c - LAG)


INTER = 1024
MT = INTER // P


def quantised_ffn(nc, a, keep):
    with ExitStack() as ctx:
        sb, ps, sem = scope(nc, ctx, "ffn0")
        x_t = keep["x_t"]
        raw_up = sb("raw_up", [P, 2, KT, INTER], I8)
        raw_down = sb("raw_down", [P, MT, E], I8)
        w_up = sb("w_up", [P, 2, KT, INTER])
        w_down = sb("w_down", [P, MT, E])
        s_up = sb("s_up", [P, 2, MT])
        s_down = sb("s_down", [P, E])
        gate = [sb(f"gate{i}", [P, CH]) for i in range(2)]
        fused = [sb(f"fused{i}", [P, MT, CH]) for i in range(2)]
        y_sb = [sb(f"y_sb{i}", [P, E]) for i in range(2)]
        g_ps = [ps(f"g{i}") for i in range(2)]
        u_ps = [ps(f"u{i}") for i in range(2)]
        y_ps = [ps(f"y{i}") for i in range(2)]
        raw_in, scales, cast_up, cast_down = (sem(n) for n in ("raw_in", "scales", "cast_up", "cast_down"))
        gated, upped, silu, fuse, made, scaled = (sem(n) for n in (
            "gated", "upped", "silu", "fuse", "made", "scaled"))
        norm = norm_parts((sb, ps, sem), keep)
        block = ctx.enter_context(nc.Block())

        @block.sync
        def _(sp):
            for j, name in enumerate(("w_gate", "w_up")):
                sp.dma_start(raw_up[:, j], a[name].bitcast(I8).rearrange("(k p) n -> p k n", p=P)).then_inc(raw_in, 16)
            sp.dma_start(raw_down[:], a["w_down"].bitcast(I8).rearrange("(k p) n -> p k n", p=P)).then_inc(raw_in, 16)
            for j, name in enumerate(("s_gate", "s_up")):
                sp.dma_start(s_up[:, j], a[name]).then_inc(scales, 16)
            sp.dma_start(s_down[:], a["s_down"].partition_broadcast(P)).then_inc(scales, 16)

        @block.gpsimd
        def _(pool):
            pool.wait_ge(raw_in, 48)
            pool.tensor_copy(w_down[:], raw_down[:]).then_inc(cast_down, 1)
            for c in range(NCH):
                norm_root(pool, norm, c)

        @block.tensor
        def _(pe):
            pe.wait_ge(cast_up, 2)

            def down(c):
                pe.wait_ge(cast_down, 1)
                for t in range(TC):
                    n = c * TC + t
                    if n >= 2:
                        pe.wait_ge(scaled, n - 1)
                    for m in range(MT):
                        pe.wait_ge(fuse, c * MT + m + 1)
                        mm = pe.matmul(y_ps[n % 2][:, 0:E], fused[c % 2][:, m, t * P:(t + 1) * P], w_down[:, m],
                                       start=(m == 0), stop=(m == MT - 1))
                    mm.then_inc(made, 1)

            for c in range(NCH + 1):
                if c < NCH:
                    for m in range(MT):
                        n = c * MT + m
                        for j, (bank, free, done) in enumerate(((g_ps, silu, gated), (u_ps, fuse, upped))):
                            if n >= 2:
                                pe.wait_ge(free, n - 1)
                            for k in range(KT):
                                mm = pe.matmul(bank[n % 2][:], w_up[:, j, k, m * P:(m + 1) * P],
                                               x_t[:, k, c * CH:(c + 1) * CH], start=(k == 0), stop=(k == KT - 1))
                            mm.then_inc(done, 1)
                if c >= 1:
                    down(c - 1)
                if c >= 2:
                    norm_turn(pe, norm, c - 2)
            norm_turn(pe, norm, NCH - 1)

        @block.scalar
        def _(act):
            act.wait_ge(scales, 48)
            for c in range(NCH + 2):
                if c < NCH:
                    for m in range(MT):
                        n = c * MT + m
                        act.wait_ge(gated, n + 1)
                        if n >= 2:
                            act.wait_ge(fuse, n - 1)
                        act.activation(gate[n % 2][:], g_ps[n % 2][:], ACT.Silu,
                                       scale=s_up[:, 0, m:m + 1]).then_inc(silu, 1)
                if c >= 2:
                    norm_keep(act, norm, c - 2)

        @block.vector
        def _(dve):
            dve.wait_ge(raw_in, 48)
            for j in range(2):
                dve.tensor_copy(w_up[:, j], raw_up[:, j]).then_inc(cast_up, 1)
            dve.wait_ge(scales, 48)

            def close(c):
                for t in range(c * TC, (c + 1) * TC):
                    dve.wait_ge(made, t + 1)
                    if t >= 2:
                        dve.wait_ge(norm["summed"], t - 1)
                    dve.tensor_tensor(y_sb[t % 2][:], y_ps[t % 2][:, 0:E], s_down[:], ALU.mult).then_inc(scaled, 1)
                    dve.wait_ge(scaled, t + 1)
                    norm_add(dve, norm, t, y_sb[t % 2][:])
                norm_measure(dve, norm, c)
                norm_scale(dve, norm, c)

            for c in range(NCH + 1):
                if c < NCH:
                    for m in range(MT):
                        n = c * MT + m
                        dve.wait_ge(upped, n + 1)
                        dve.wait_ge(silu, n + 1)
                        if c >= 2:
                            dve.wait_ge(made, (c - 1) * TC)
                        dve.scalar_tensor_tensor(out=fused[c % 2][:, m], in0=u_ps[n % 2][:],
                                                 scalar=s_up[:, 1, m:m + 1], in1=gate[n % 2][:],
                                                 op0=ALU.mult, op1=ALU.mult).then_inc(fuse, 1)
                if c >= 1:
                    close(c - 1)


H1, D1 = 4, 64
ROT = D1 // 2


def retention_tables():
    import numpy as np
    inv = 1.0 / 10000.0 ** (np.arange(0, ROT, 2, dtype=np.float64) / ROT)
    t = np.arange(SEQ, dtype=np.float64)
    freqs = np.repeat(t[:, None] * inv[None, :], 2, axis=-1)
    base = (np.arange(0, ROT, 2, dtype=np.float64) + 0.4 * ROT) / (1.4 * ROT)
    scale = base[None, :] ** ((t - SEQ // 2) / 512.0)[:, None]
    scale = np.concatenate([scale, scale], axis=-1)
    sign = np.where(np.arange(ROT) % 2 == 0, -1.0, 1.0)
    out = np.zeros((2, 2, E, SEQ))
    for h in range(H1):
        decay = (1.0 - 2.0 ** (-5.0 - h)) ** t
        for side, (sc, dc) in enumerate(((scale, decay), (1.0 / scale, 1.0 / decay))):
            r = h * D1
            out[side, 0, r:r + ROT] = (np.cos(freqs) * sc).T * dc
            out[side, 1, r:r + ROT] = (np.sin(freqs) * sc * sign).T * dc
            out[side, 0, r + ROT:r + D1] = dc
    return out.astype(np.float32)


def retention(nc, a, keep):
    with ExitStack() as ctx:
        sb, ps, sem = scope(nc, ctx, "ret")
        x_t = keep["x_t"]
        w = sb("w", [P, 5, KT, E])
        tab = [sb(f"tab{i}", [P, 2, 2, CH]) for i in range(2)]
        qk_t = sb("qk_t", [P, 2, KT, TOK])
        mish = sb("mish", [P, KT, TOK])
        v = sb("v", [P, NT, E])
        k_tok = sb("k_tok", [P, NT, E])
        ret = sb("ret", [P, KT, TOK])
        raw, swapped, part = (sb(n, [P, 2, CH]) for n in ("raw", "swapped", "part"))
        g_min, g_exp, g_num = (sb(n, [P, 2, CH]) for n in ("g_min", "g_exp", "g_num"))
        causal = sb("causal", [P, 2, P])
        masked = [sb(f"masked{i}", [P, 2, 2, P]) for i in range(2)]
        state = [sb(f"state{i}", [P, KT, D1]) for i in range(2)]
        blocks1 = sb("blocks1", [P, P])
        gn = sb("gn", [P, 2, KT])
        gstat = sb("gstat", [P, KT * BATCH, 2, 6])
        gmv = sb("gmv", [P, KT * BATCH, 2])
        gtmp = sb("gtmp", [P, 6, KT * BATCH])
        banks = [ps(f"b{i}") for i in range(6)]
        norm = norm_parts((sb, ps, sem), keep)

        weights, tables = sem("weights"), [sem(f"tables{i}") for i in range(2)]
        consts = sem("consts")
        projected, raw_in, swap_done, sin_done, cos_done, rot_done = (sem(n) for n in (
            "projected", "raw_in", "swap_done", "sin_done", "cos_done", "rot_done"))
        g_made, g_raw, g_low, g_e, g_n, g_d, g_r, g_q, g_done = (sem(n) for n in (
            "g_made", "g_raw", "g_low", "g_e", "g_n", "g_d", "g_r", "g_q", "g_done"))
        v_made, v_in, k_turned, k_in = (sem(n) for n in ("v_made", "v_in", "k_turned", "k_in"))
        scored, mask_done, state_made, state_in, ret_made, ret_in = (sem(n) for n in (
            "scored", "mask_done", "state_made", "state_in", "ret_made", "ret_in"))
        gchain, gsq, ggroup, groot, gpow = (sem(n) for n in ("gchain", "gsq", "ggroup", "groot", "gpow"))
        applied, weighed, made = (sem(n) for n in ("applied", "weighed", "made"))

        rot = [(c, side, m) for c in range(NCH) for m in range(KT) for side in range(2)]
        gates = [(c, m) for c in range(NCH) for m in range(KT)]
        block = ctx.enter_context(nc.Block())

        @block.sync
        def _(sp):
            for i, name in enumerate(("w_q1", "w_k1", "w_g1", "w_v1", "w_o1")):
                sp.dma_start(w[:, i], a[name].rearrange("(k p) n -> p k n", p=P)).then_inc(weights, 16)
            for n in range(NCH * KT):
                c, m = n // KT, n % KT
                if n >= 2:
                    sp.wait_ge(cos_done, 2 * (n - 1))
                    sp.wait_ge(sin_done, 2 * (n - 1))
                cc = c % QC
                for side in range(2):
                    sp.dma_start(tab[n % 2][:, side],
                                 a["tables"][side, :, m * P:(m + 1) * P, cc * CH:(cc + 1) * CH]
                                 .rearrange("f p t -> p f t")).then_inc(tables[n % 2], 16)
            sp.dma_start(gn[:, 0], a["gn_w"]).then_inc(consts, 16)
            sp.dma_start(gn[:, 1], a["gn_b"]).then_inc(consts, 16)

        @block.gpsimd
        def _(pool):
            pool.memset(causal[:], 1.0).then_inc(groot, 1)
            pool.memset(blocks1[:], 0.0).then_inc(groot, 1)
            pool.wait_ge(groot, 2)
            pool.affine_select(out=causal[:], in_=causal[:], compare_op=ALU.is_ge, fill=0.0,
                               base=0, pattern=[[0, 2], [1, P]], channel_multiplier=-1).then_inc(groot, 1)
            for i in range(2):
                pool.wait_ge(groot, 3 + i)
                pool.memset(blocks1[i * D1:(i + 1) * D1, i * D1:(i + 1) * D1], 1.0 / D1).then_inc(groot, 1)
            pool.wait_ge(groot, 5)
            for n, (c, side, m) in enumerate(rot):
                pool.wait_ge(cos_done, n + 1)
                pool.wait_ge(sin_done, n + 1)
                pool.tensor_tensor(qk_t[:, side, m, c * CH:(c + 1) * CH], part[:, n % 2], swapped[:, n % 2],
                                   ALU.add).then_inc(rot_done, 1)
            for n, (c, m) in enumerate(gates):
                pool.wait_ge(g_r, n + 1)
                pool.tensor_tensor(g_num[:, n % 2], g_num[:, n % 2], g_exp[:, n % 2], ALU.mult).then_inc(g_q, 1)
            pool.wait_ge(gsq, 6)
            pool.tensor_tensor(gtmp[:, 3], gtmp[:, 2], norm["half"][:, 0:KT * BATCH], ALU.pow).then_inc(gpow, 1)
            for c in range(NCH):
                norm_root(pool, norm, c)

        @block.tensor
        def _(pe):
            pe.wait_ge(weights, 80)
            for n, (c, side, m) in enumerate(rot):
                if n >= 2:
                    pe.wait_ge(cos_done, n - 1)
                    pe.wait_ge(raw_in, n - 1)
                for k in range(KT):
                    mm = pe.matmul(banks[n % 2][:], w[:, side, k, m * P:(m + 1) * P],
                                   x_t[:, k, c * CH:(c + 1) * CH], start=(k == 0), stop=(k == KT - 1))
                mm.then_inc(projected, 1)
            for n, (c, m) in enumerate(gates):
                if n >= 2:
                    pe.wait_ge(g_low, n - 1)
                for k in range(KT):
                    mm = pe.matmul(banks[2 + n % 2][:], w[:, 2, k, m * P:(m + 1) * P],
                                   x_t[:, k, c * CH:(c + 1) * CH], start=(k == 0), stop=(k == KT - 1))
                mm.then_inc(g_made, 1)
            for t in range(NT):
                if t >= 2:
                    pe.wait_ge(v_in, t - 1)
                for k in range(KT):
                    mm = pe.matmul(banks[4 + t % 2][:, 0:E], x_t[:, k, t * P:(t + 1) * P], w[:, 3, k],
                                   start=(k == 0), stop=(k == KT - 1))
                mm.then_inc(v_made, 1)
            pe.wait_ge(rot_done, len(rot))
            for t in range(NT):
                if t >= 2:
                    pe.wait_ge(k_in, t - 1)
                for m in range(KT):
                    mm = pe.transpose(banks[t % 2][:, m * P:(m + 1) * P], qk_t[:, 1, m, t * P:(t + 1) * P],
                                      keep["ident"][:])
                mm.then_inc(k_turned, 1)
            pe.wait_ge(v_in, NT)
            pe.wait_ge(k_in, NT)
            pe.wait_ge(g_low, len(gates))

            def scores(t):
                if t >= 1:
                    pe.wait_ge(mask_done, 2 * t)
                for h in range(H1):
                    r, m = D1 * (h % 2), h // 2
                    mm = pe.matmul(banks[h % 2][:, m * P:(m + 1) * P], qk_t[r:r + D1, 1, m, t * P:(t + 1) * P],
                                   qk_t[r:r + D1, 0, m, t * P:(t + 1) * P], start=True, stop=True)
                mm.then_inc(scored, 1)

            scores(0)
            for t in range(NT):
                n = t % KTS
                if t + 1 < NT:
                    scores(t + 1)
                pe.wait_ge(mask_done, 2 * t + 2)
                if t:
                    pe.wait_ge(ret_in, 2 * t)
                if n:
                    pe.wait_ge(state_in, t)
                for h in range(H1):
                    r, m = D1 * (h % 2), h // 2
                    out = banks[2 + h % 2][r:r + D1, m * P:(m + 1) * P]
                    mm = pe.matmul(out, v[:, t, h * D1:(h + 1) * D1], masked[t % 2][:, h % 2, m],
                                   start=True, stop=(n == 0))
                    if n:
                        mm = pe.matmul(out, state[(t - 1) % 2][r:r + D1, m], qk_t[r:r + D1, 0, m, t * P:(t + 1) * P],
                                       start=False, stop=True)
                mm.then_inc(ret_made, 1)
                if t:
                    pe.wait_ge(state_in, t)
                for h in range(H1):
                    r, m = D1 * (h % 2), h // 2
                    mm = pe.matmul(banks[4 + m][r:r + D1, 0:D1], k_tok[:, t, h * D1:(h + 1) * D1],
                                   v[:, t, h * D1:(h + 1) * D1], start=(n == 0), stop=(n == KTS - 1),
                                   skip_group_check=True)
                mm.then_inc(state_made, 1)
            pe.wait_ge(gsq, 2)
            pe.matmul(banks[0][:, 0:2 * KT * BATCH], blocks1[:], gmv[:].rearrange("p a b -> p (a b)"),
                      start=True, stop=True).then_inc(ggroup, 1)
            for c in range(NCH + LAG):
                if c < NCH:
                    for t in range(c * TC, (c + 1) * TC):
                        b = t // KTS
                        pe.wait_ge(weighed, KT * (b + 1))
                        if t >= 2:
                            pe.wait_ge(norm["summed"], t - 1)
                        for k in range(KT):
                            mm = pe.matmul(banks[4 + t % 2][:, 0:E], ret[:, k, t * P:(t + 1) * P], w[:, 4, k],
                                           start=(k == 0), stop=(k == KT - 1))
                        mm.then_inc(made, 1)
                if c >= LAG:
                    norm_turn(pe, norm, c - LAG)

        @block.scalar
        def _(act):
            for n, (c, side, m) in enumerate(rot):
                act.wait_ge(projected, n + 1)
                if n >= 2:
                    act.wait_ge(swap_done, n - 1)
                act.activation(raw[:, n % 2], banks[n % 2][:], ACT.Copy).then_inc(raw_in, 1)
            for n, (c, m) in enumerate(gates):
                act.wait_ge(g_made, n + 1)
                act.activation(mish[:, m, c * CH:(c + 1) * CH], banks[2 + n % 2][:], ACT.Copy).then_inc(g_raw, 1)
                act.wait_ge(g_low, n + 1)
                if n >= 2:
                    act.wait_ge(g_q, n - 1)
                act.activation(g_exp[:, n % 2], g_min[:, n % 2], ACT.Exp).then_inc(g_e, 1)
            for t in range(NT):
                act.wait_ge(v_made, t + 1)
                act.activation(v[:, t], banks[4 + t % 2][:, 0:E], ACT.Copy).then_inc(v_in, 1)
            for t in range(NT):
                act.wait_ge(k_turned, t + 1)
                act.activation(k_tok[:, t], banks[t % 2][:, 0:E], ACT.Copy).then_inc(k_in, 1)
            for t in range(NT):
                act.wait_ge(ret_made, t + 1)
                for i in range(2):
                    r = D1 * i
                    act.activation(ret[r:r + D1, :, t * P:(t + 1) * P],
                                   banks[2 + i][r:r + D1, 0:KT * P].rearrange("p (m t) -> p m t", m=KT),
                                   ACT.Copy).then_inc(ret_in, 1)
            for c in range(NCH):
                norm_keep(act, norm, c)

        @block.vector
        def _(dve):
            swap = [i ^ 1 for i in range(32)]
            for n, (c, side, m) in enumerate(rot):
                dve.wait_ge(raw_in, n + 1)
                if n >= 2:
                    dve.wait_ge(rot_done, n - 1)
                dve.stream_shuffle(swapped[:, n % 2], raw[:, n % 2], swap).then_inc(swap_done, 1)
                dve.wait_ge(tables[(n // 2) % 2], 32 * (n // 4 + 1))
                dve.tensor_tensor(part[:, n % 2], banks[n % 2][:], tab[(n // 2) % 2][:, side, 0],
                                  ALU.mult).then_inc(cos_done, 1)
                dve.wait_ge(swap_done, n + 1)
                dve.tensor_tensor(swapped[:, n % 2], swapped[:, n % 2], tab[(n // 2) % 2][:, side, 1],
                                  ALU.mult).then_inc(sin_done, 1)
            for n, (c, m) in enumerate(gates):
                dve.wait_ge(g_raw, n + 1)
                if n >= 2:
                    dve.wait_ge(g_e, n - 1)
                dve.tensor_scalar(g_min[:, n % 2], banks[2 + n % 2][:], 20.0, None, ALU.min).then_inc(g_low, 1)
                dve.wait_ge(g_e, n + 1)
                if n >= 2:
                    dve.wait_ge(g_done, n - 1)
                dve.scalar_tensor_tensor(out=g_num[:, n % 2], in0=g_exp[:, n % 2], scalar=2.0, in1=g_exp[:, n % 2],
                                         op0=ALU.add, op1=ALU.mult).then_inc(g_n, 1)
                dve.wait_ge(g_n, n + 1)
                dve.tensor_scalar(g_exp[:, n % 2], g_num[:, n % 2], 2.0, None, ALU.add).then_inc(g_d, 1)
                dve.wait_ge(g_d, n + 1)
                dve.reciprocal(g_exp[:, n % 2], g_exp[:, n % 2]).then_inc(g_r, 1)
                dve.wait_ge(g_q, n + 1)
                dve.tensor_tensor(mish[:, m, c * CH:(c + 1) * CH], mish[:, m, c * CH:(c + 1) * CH],
                                  g_num[:, n % 2], ALU.mult).then_inc(g_done, 1)
            dve.wait_ge(groot, 5)
            for t in range(NT):
                dve.wait_ge(scored, t + 1)
                if t >= 2:
                    dve.wait_ge(ret_made, t - 1)
                for i in range(2):
                    dve.tensor_tensor(masked[t % 2][:, i], banks[i][:, 0:KT * P].rearrange("p (m t) -> p m t", m=KT),
                                      causal[:], ALU.mult).then_inc(mask_done, 1)
                dve.wait_ge(state_made, t + 1)
                if t >= 2:
                    dve.wait_ge(ret_made, t)
                for m in range(KT):
                    cp = dve.tensor_copy(state[t % 2][:, m], banks[4 + m][:, 0:D1])
                cp.then_inc(state_in, 1)
            for b in range(BATCH):
                for m in range(KT):
                    i = b * KT + m
                    dve.wait_ge(ret_in, 2 * KTS * (b + 1))
                    for c in range(QC):
                        st = dve.bn_stats(gstat[:, i, c], ret[:, m, b * SEQ + c * CH:b * SEQ + (c + 1) * CH])
                    st.then_inc(gchain, 1)
            for i in range(KT * BATCH):
                dve.wait_ge(gchain, i + 1)
                ag = dve.bn_aggr(gmv[:, i], gstat[:, i].rearrange("p a b -> p (a b)"))
            ag.then_inc(gchain, 1)
            dve.wait_ge(gchain, KT * BATCH + 1)
            mean, var = gmv[:, :, 0], gmv[:, :, 1]
            dve.tensor_tensor(gtmp[:, 0], mean, mean, ALU.mult).then_inc(gsq, 1)
            dve.wait_ge(gsq, 1)
            dve.tensor_tensor(var, var, gtmp[:, 0], ALU.add).then_inc(gsq, 1)
            dve.wait_ge(ggroup, 1)
            group = banks[0][:, 0:2 * KT * BATCH].rearrange("p (a b) -> p a b", b=2)
            dve.tensor_copy(gtmp[:, 1], group[:, :, 0]).then_inc(gsq, 1)
            dve.wait_ge(gsq, 3)
            dve.tensor_tensor(gtmp[:, 0], gtmp[:, 1], gtmp[:, 1], ALU.mult).then_inc(gsq, 1)
            dve.wait_ge(gsq, 4)
            dve.tensor_tensor(gtmp[:, 2], group[:, :, 1], gtmp[:, 0], ALU.subtract).then_inc(gsq, 1)
            dve.wait_ge(gsq, 5)
            dve.tensor_scalar(gtmp[:, 2], gtmp[:, 2], 0.0, EPS, ALU.max, ALU.add).then_inc(gsq, 1)
            dve.wait_ge(gpow, 1)
            dve.wait_ge(consts, 32)
            for b in range(BATCH):
                dve.tensor_tensor(gtmp[:, 4, b * KT:(b + 1) * KT], gtmp[:, 3, b * KT:(b + 1) * KT], gn[:, 0],
                                  ALU.mult).then_inc(gsq, 1)
            dve.wait_ge(gsq, 8)
            dve.tensor_tensor(gtmp[:, 0], gtmp[:, 1], gtmp[:, 4], ALU.mult).then_inc(gsq, 1)
            dve.wait_ge(gsq, 9)
            for b in range(BATCH):
                dve.tensor_tensor(gtmp[:, 5, b * KT:(b + 1) * KT], gn[:, 1], gtmp[:, 0, b * KT:(b + 1) * KT],
                                  ALU.subtract).then_inc(gsq, 1)
            dve.wait_ge(gsq, 11)
            dve.wait_ge(g_done, len(gates))
            for b in range(BATCH):
                for m in range(KT):
                    i = b * KT + m
                    r = ret[:, m, b * SEQ:(b + 1) * SEQ]
                    dve.tensor_scalar(r, r, gtmp[:, 4, i:i + 1], gtmp[:, 5, i:i + 1], ALU.mult,
                                      ALU.add).then_inc(applied, 1)
                    dve.wait_ge(applied, i + 1)
                    dve.tensor_tensor(r, r, mish[:, m, b * SEQ:(b + 1) * SEQ], ALU.mult).then_inc(weighed, 1)
            for c in range(NCH):
                for t in range(c * TC, (c + 1) * TC):
                    dve.wait_ge(made, t + 1)
                    norm_add(dve, norm, t, banks[4 + t % 2][:, 0:E])
                norm_measure(dve, norm, c)
                norm_scale(dve, norm, c)


EXPERTS, TOP, WIDE = 64, 6, 176
HALF = WIDE // 2
HPAD = 96
SHARED = 2 * WIDE
SH_TILES = (128, 128, 96)
TILES = -(-(TOK * TOP // P + EXPERTS) // 8) * 8
assert sum(SH_TILES) == SHARED


def route(nc, a, keep):
    with ExitStack() as ctx:
        sb, ps, sem = scope(nc, ctx, "route")
        x, x_t = keep["x"], keep["x_t"]
        weight, slot_i, tok_i, owner, y_sh = (keep[n] for n in ("weight", "slot_i", "tok_i", "owner", "y_sh"))
        w_r = sb("w_r", [P, KT, EXPERTS])
        w_up = sb("w_up", [P, KT, 2 * SHARED])
        w_down = sb("w_down", [P, len(SH_TILES), E])
        logit = sb("logit", [P, NT, EXPERTS])
        best = sb("best", [P, NT, 8])
        best_i = sb("best_i", [P, NT, 8], U32)
        best_f = sb("best_f", [P, NT, 8])
        expo = sb("expo", [P, NT, TOP])
        esum = sb("esum", [P, NT])
        iota = sb("iota", [P, TILES])
        lane = sb("lane", [P, 1])
        tile_no = sb("tile_no", [P, 2])
        chosen = sb("chosen", [P, TOP, NT, EXPERTS], BF16)
        member = sb("member", [P, NT, EXPERTS], BF16)
        sums = sb("sums", [P, NT + 1, EXPERTS], BF16)
        before = sb("before", [P, P], BF16)
        upto = sb("upto", [P, P], BF16)
        ones = sb("ones", [P, P], BF16)
        count_i = sb("count_i", [EXPERTS, 2], I32)
        n_tiles = sb("n_tiles", [EXPERTS, P], BF16)
        base = sb("base", [P, EXPERTS])
        ends = sb("ends", [P, EXPERTS])
        place = sb("place", [P, NT, EXPERTS])
        pick = sb("pick", [P, NT, EXPERTS])
        slot = sb("slot", [P, NT, TOP])
        low_i, high_i = sb("low_i", [P, NT, TOP], I32), sb("high_i", [P, NT, TOP], I32)
        low, high = sb("low", [P, NT, TOP]), sb("high", [P, NT, TOP])
        HOTS = 16
        hot_low = sb("hot_low", [P, HOTS, P], BF16)
        hot_high = sb("hot_high", [P, HOTS, 2, TILES], BF16)
        tok_f = sb("tok_f", [P, TILES])
        past = sb("past", [P, 2, EXPERTS])
        owner_f, owner_i = sb("owner_f", [P, 2]), sb("owner_i", [P, 2], I32)
        sh_gate = [sb(f"sh_gate{i}", [P, CH]) for i in range(2)]
        sh_h = [sb(f"sh_h{i}", [P, len(SH_TILES), CH]) for i in range(2)]
        l_ps = [ps(f"l{i}") for i in range(2)]
        g_ps = [ps(f"g{i}") for i in range(2)]
        u_ps = [ps(f"u{i}") for i in range(2)]
        y_ps = ps("y")
        m_ps = ps("m")
        w_in, w_r_in, x_out = sem("w_in"), sem("w_r_in"), sem("x_out")
        consts, lg_made, lg_in, best_in, bi_in, vc = (sem(n) for n in (
            "consts", "lg_made", "lg_in", "best_in", "bi_in", "vc"))
        exp_in, placed, counted, based, owned, owner_out, owner_in = (sem(n) for n in (
            "exp_in", "placed", "counted", "based", "owned", "owner_out", "owner_in"))
        hot_in, hot_used = sem("hot_in"), sem("hot_used")
        gated, upped, silu, fuse, made, y_in = (sem(n) for n in ("gated", "upped", "silu", "fuse", "made", "y_in"))
        PER_BANK = CH // EXPERTS
        pairs = [(t, k) for t in range(NT) for k in range(TOP)]
        ST = len(SH_TILES)
        A_VC = 8 + TOP - 1 + NT
        block = ctx.enter_context(nc.Block())

        @block.sync
        def _(sp):
            sp.dma_start(w_r[:], a["w_router"].rearrange("(k p) n -> p k n", p=P)).then_inc(w_r_in, 16)
            sp.dma_start(w_up[:], a["w_sh_up"].rearrange("(k p) n -> p k n", p=P)).then_inc(w_in, 16)
            for m, rows in enumerate(SH_TILES):
                sp.dma_start(w_down[0:rows, m], a["w_sh_down"][m * P:m * P + rows]).then_inc(w_in, 16)
            sp.dma_start(a["x_rows"].rearrange("(t p) n -> p t n", p=P), x[:]).then_inc(x_out, 16)
            sp.wait_ge(owned, 1)
            sp.dma_start(a["owners"].rearrange("(p a) -> p a", p=P), owner_i[:]).then_inc(owner_out, 16)
            sp.wait_ge(owner_out, 16)
            sp.dma_start(owner[:], a["owners"].rearrange("(o n) -> o n", o=1)).then_inc(owner_in, 16)
            sp.wait_ge(owner_in, 16)
            sp.wait_ge(x_out, 16)

        @block.gpsimd
        def _(pool):
            done = 0

            def ordered(instruction):
                nonlocal done
                instruction.then_inc(consts, 1)
                done += 1
                pool.wait_ge(consts, done)

            ordered(pool.iota(iota[:], pattern=[[1, TILES]], base=0, channel_multiplier=0,
                              allow_small_or_imprecise_dtypes=True))
            ordered(pool.iota(lane[:], pattern=[[1, 1]], base=0, channel_multiplier=1,
                              allow_small_or_imprecise_dtypes=True))
            ordered(pool.iota(tile_no[:], pattern=[[1, 2]], base=0, channel_multiplier=2,
                              allow_small_or_imprecise_dtypes=True))
            ordered(pool.memset(ones[:], 1.0))
            ordered(pool.memset(before[:], 1.0))
            ordered(pool.memset(upto[:], 1.0))
            ordered(pool.affine_select(out=before[:], in_=before[:], compare_op=ALU.is_gt, fill=0.0,
                                       base=0, pattern=[[1, P]], channel_multiplier=-1))
            ordered(pool.affine_select(out=upto[:], in_=upto[:], compare_op=ALU.is_ge, fill=0.0,
                                       base=0, pattern=[[1, P]], channel_multiplier=-1))
            ordered(pool.memset(sums[:, 0], 0.0))

        @block.tensor
        def _(pe):
            pe.wait_ge(w_r_in, 16)
            for t in range(NT):
                for k in range(KT):
                    mm = pe.matmul(l_ps[t // PER_BANK][:, t % PER_BANK * EXPERTS:(t % PER_BANK + 1) * EXPERTS],
                                   x_t[:, k, t * P:(t + 1) * P], w_r[:, k], start=(k == 0), stop=(k == KT - 1))
                mm.then_inc(lg_made, 1)

            pe.wait_ge(w_in, 16 * (1 + ST))

            def shared_up(c):
                for m, rows in enumerate(SH_TILES):
                    n = c * ST + m
                    for j, (bank, free, done) in enumerate(((g_ps, silu, gated), (u_ps, fuse, upped))):
                        if n >= 2:
                            pe.wait_ge(free, n - 1)
                        for k in range(KT):
                            col = j * SHARED + m * P
                            mm = pe.matmul(bank[n % 2][0:rows, :], w_up[:, k, col:col + rows],
                                           x_t[:, k, c * CH:(c + 1) * CH], start=(k == 0), stop=(k == KT - 1))
                        mm.then_inc(done, 1)

            def shared_down(c):
                for t in range(c * TC, (c + 1) * TC):
                    if t:
                        pe.wait_ge(y_in, t)
                    for m, rows in enumerate(SH_TILES):
                        pe.wait_ge(fuse, c * ST + m + 1)
                        mm = pe.matmul(y_ps[:, 0:E], sh_h[c % 2][0:rows, m, t % TC * P:(t % TC + 1) * P],
                                       w_down[0:rows, m], start=(m == 0), stop=(m == ST - 1))
                    mm.then_inc(made, 1)

            shared_up(0)
            pe.wait_ge(consts, 9)
            pe.wait_ge(vc, A_VC)
            pe.wait_ge(lg_in, 2)
            for t in range(NT):
                out = l_ps[t // PER_BANK][:, t % PER_BANK * EXPERTS:(t % PER_BANK + 1) * EXPERTS]
                pe.matmul(out, before[:], member[:, t], start=True, stop=False)
                mm = pe.matmul(out, ones[:], sums[:, t], start=False, stop=True)
            mm.then_inc(placed, 1)
            pe.matmul(m_ps[0:EXPERTS, 0:1], sums[:, NT], ones[:, 0:1], start=True, stop=True).then_inc(counted, 1)
            shared_up(1)
            pe.wait_ge(vc, A_VC + 3)
            pe.matmul(m_ps[:, 0:EXPERTS], n_tiles[:], before[0:EXPERTS, 0:EXPERTS], start=True, stop=True)
            pe.matmul(m_ps[:, EXPERTS:2 * EXPERTS], n_tiles[:], upto[0:EXPERTS, 0:EXPERTS],
                      start=True, stop=True).then_inc(based, 1)
            shared_down(0)
            for c in range(2, NCH):
                shared_up(c)
                shared_down(c - 1)
            shared_down(NCH - 1)
            pe.wait_ge(vc, A_VC + 5)
            for n, (t, k) in enumerate(pairs):
                pe.wait_ge(hot_in, n + 1)
                pe.matmul(m_ps[:, 0:2 * TILES], hot_low[:, n % HOTS],
                          hot_high[:, n % HOTS].rearrange("p a j -> p (a j)"),
                          start=(n == 0), stop=(n == len(pairs) - 1)).then_inc(hot_used, 1)

        @block.scalar
        def _(act):
            for i in range(2):
                act.wait_ge(lg_made, PER_BANK * (i + 1))
                act.activation(logit[:, i * PER_BANK:(i + 1) * PER_BANK], l_ps[i][:].rearrange(
                    "p (t e) -> p t e", e=EXPERTS), ACT.Copy).then_inc(lg_in, 1)

            act.wait_ge(vc, 3)
            act.activation(expo[:], expo[:], ACT.Exp).then_inc(exp_in, 1)
            for c in range(NCH):
                for m, rows in enumerate(SH_TILES):
                    n = c * ST + m
                    act.wait_ge(gated, n + 1)
                    if n >= 2:
                        act.wait_ge(fuse, n - 1)
                    act.activation(sh_gate[n % 2][0:rows], g_ps[n % 2][0:rows, :], ACT.Silu).then_inc(silu, 1)
                if c >= 1:
                    for t in range((c - 1) * TC, c * TC):
                        act.wait_ge(made, t + 1)
                        act.activation(y_sh[:, t], y_ps[:, 0:E], ACT.Copy).then_inc(y_in, 1)
            for t in range((NCH - 1) * TC, NT):
                act.wait_ge(made, t + 1)
                act.activation(y_sh[:, t], y_ps[:, 0:E], ACT.Copy).then_inc(y_in, 1)

        @block.vector
        def _(dve):
            steps = 0

            def chain(instruction):
                nonlocal steps
                instruction.then_inc(vc, 1)
                steps += 1
                dve.wait_ge(vc, steps)

            def fuse_shared(c):
                for m, rows in enumerate(SH_TILES):
                    n = c * ST + m
                    dve.wait_ge(upped, n + 1)
                    dve.wait_ge(silu, n + 1)
                    if c >= 2:
                        dve.wait_ge(made, (c - 1) * TC)
                    dve.tensor_tensor(sh_h[c % 2][0:rows, m], u_ps[n % 2][0:rows, :], sh_gate[n % 2][0:rows],
                                      ALU.mult).then_inc(fuse, 1)

            for t in range(NT):
                dve.wait_ge(lg_in, t // PER_BANK + 1)
                dve.max(best[:, t], logit[:, t]).then_inc(best_in, 1)
            for t in range(NT):
                dve.wait_ge(best_in, t + 1)
                dve.max_index(best_i[:, t], best[:, t], logit[:, t]).then_inc(bi_in, 1)
            dve.wait_ge(bi_in, NT)
            chain(dve.tensor_copy(best_f[:], best_i[:]))
            dve.wait_ge(consts, 9)
            chain(dve.memset(esum[:], 0.0))
            chain(dve.tensor_tensor(expo[:], best[:, :, 0:TOP], best[:, :, 0:1].to_broadcast([P, NT, TOP]),
                                    ALU.subtract))
            dve.wait_ge(exp_in, 1)
            chain(dve.tensor_reduce(esum[:], expo[:], AX.X, ALU.add))
            chain(dve.reciprocal(esum[:], esum[:]))
            chain(dve.tensor_tensor(weight[:], expo[:], esum[:].unsqueeze(2).to_broadcast([P, NT, TOP]), ALU.mult))
            for k in range(TOP):
                op = dve.tensor_tensor(chosen[:, k], iota[:, 0:EXPERTS].unsqueeze(1).to_broadcast([P, NT, EXPERTS]),
                                       best_f[:, :, k:k + 1].to_broadcast([P, NT, EXPERTS]), ALU.is_equal)
            chain(op)
            chain(dve.tensor_copy(member[:], chosen[:, 0]))
            for k in range(1, TOP):
                chain(dve.tensor_tensor(member[:], member[:], chosen[:, k], ALU.add))
            for t in range(NT):
                chain(dve.tensor_tensor(sums[:, t + 1], sums[:, t], member[:, t], ALU.add))
            assert steps == A_VC
            fuse_shared(0)
            dve.wait_ge(counted, 1)
            chain(dve.tensor_scalar(count_i[:, 0:1], m_ps[0:EXPERTS, 0:1], float(P - 1), None, ALU.add))
            chain(dve.tensor_single_scalar(count_i[:, 1:2], count_i[:, 0:1], 7, ALU.logical_shift_right))
            chain(dve.tensor_copy(n_tiles[:], count_i[:, 1:2].to_broadcast([EXPERTS, P])))
            fuse_shared(1)
            dve.wait_ge(based, 1)
            chain(dve.tensor_scalar(base[:], m_ps[:, 0:EXPERTS], float(P), None, ALU.mult))
            chain(dve.tensor_copy(ends[:], m_ps[:, EXPERTS:2 * EXPERTS]))
            for i in range(2):
                chain(dve.tensor_scalar(past[:, i], ends[:], tile_no[:, i:i + 1], None, ALU.is_le))
            chain(dve.tensor_reduce(owner_f[:], past[:], AX.X, ALU.add))
            chain(dve.tensor_scalar(owner_f[:], owner_f[:], float(EXPERTS - 1), None, ALU.min))
            dve.tensor_copy(owner_i[:], owner_f[:]).then_inc(owned, 1)
            for c in range(2, NCH):
                fuse_shared(c)
            dve.wait_ge(placed, 1)
            for i in range(2):
                chain(dve.tensor_tensor(place[:, i * PER_BANK:(i + 1) * PER_BANK],
                                        l_ps[i][:].rearrange("p (t e) -> p t e", e=EXPERTS),
                                        base[:].unsqueeze(1).to_broadcast([P, PER_BANK, EXPERTS]), ALU.add))
            for k in range(TOP):
                chain(dve.tensor_tensor(pick[:], place[:], chosen[:, k], ALU.mult))
                chain(dve.tensor_reduce(slot[:, :, k], pick[:], AX.X, ALU.add))
            chain(dve.tensor_copy(slot_i[:], slot[:]))
            chain(dve.tensor_single_scalar(low_i[:], slot_i[:], P - 1, ALU.bitwise_and))
            chain(dve.tensor_single_scalar(high_i[:], slot_i[:], 7, ALU.logical_shift_right))
            chain(dve.tensor_copy(low[:], low_i[:]))
            chain(dve.tensor_copy(high[:], high_i[:]))
            for n, (t, k) in enumerate(pairs):
                if n >= HOTS:
                    dve.wait_ge(hot_used, n - HOTS + 1)
                dve.tensor_scalar(hot_low[:, n % HOTS], iota[:, 0:P], low[:, t, k:k + 1], None, ALU.is_equal)
                dve.tensor_scalar(hot_high[:, n % HOTS, 0], iota[:], high[:, t, k:k + 1], float(t),
                                  ALU.is_equal, ALU.mult)
                dve.tensor_scalar(hot_high[:, n % HOTS, 1], iota[:], high[:, t, k:k + 1], lane[:, 0:1],
                                  ALU.is_equal, ALU.mult).then_inc(hot_in, 1)
            dve.wait_ge(hot_used, len(pairs))
            chain(dve.tensor_scalar(tok_f[:], m_ps[:, 0:TILES], float(P), None, ALU.mult))
            chain(dve.tensor_tensor(tok_f[:], m_ps[:, TILES:2 * TILES], tok_f[:], ALU.add))
            chain(dve.tensor_copy(tok_i[:], tok_f[:]))
            dve.wait_ge(y_in, NT)
            dve.wait_ge(x_out, 16)
            chain(dve.tensor_tensor(x[:], x[:], y_sh[:], ALU.add))


def experts(nc, a, keep):
    with ExitStack() as ctx:
        sb, ps, sem = scope(nc, ctx, "exp")
        tok_i, owner, ident = keep["tok_i"], keep["owner"], keep["ident"]
        UN = 8
        B = 4
        TURNS = TILES // UN
        w1 = [sb(f"w1_{i}", [P, KT, 2, HALF]) for i in range(B)]
        w2 = [sb(f"w2_{i}", [HPAD, 2, E]) for i in range(B)]
        idx = [sb(f"idx{i}", [P, B], I32) for i in range(UN // B)]
        spare = sb("spare", [P, 1])
        rows = [sb(f"rows{i}", [P, E]) for i in range(B)]
        xt = [sb(f"xt{i}", [P, KT, P]) for i in range(2)]
        ht = [sb(f"ht{i}", [HPAD, 2, P]) for i in range(2)]
        y_sb = [sb(f"y_sb{i}", [P, E]) for i in range(B)]
        xt_ps = [ps(f"xt_ps{i}") for i in range(2)]
        h_ps = [ps(f"h_ps{i}") for i in range(2)]
        y_ps = [ps(f"y_ps{i}") for i in range(2)]
        w_in = [sem(f"w_in{i}") for i in range(B)]
        turned = [sem(f"turned{i}") for i in range(B)]
        y_made = [sem(f"y_made{i}") for i in range(B)]
        rows_in = [sem(f"rows_in{i}") for i in range(B)]
        y_out = [sem(f"y_out{i}") for i in range(B)]
        padded, idx_in, stepped = sem("padded"), sem("idx_in"), sem("stepped")
        xt_in, h_made, h_in, y_in = (sem(n) for n in ("xt_in", "h_made", "h_in", "y_in"))
        block = ctx.enter_context(nc.Block())

        def nth(i, b):
            return i * (UN // B) + b // B

        @block.sync
        def _(sp):
            sp.wait_ge(padded, 2 + B)
            with sp.Fori(0, TURNS) as i:
                for b in range(UN):
                    n = b % B
                    e = sp.value_load(owner[0:1, bass.ds(i * UN + b, 1)], min_val=0, max_val=EXPERTS - 1)
                    sp.wait_ge(y_made[n], nth(i, b))
                    sp.dma_start(w1[n][:], a["w1"][e].rearrange("p (k j n) -> p k j n", k=KT, j=2)
                                 ).then_inc(w_in[n], 16)
                    sp.dma_start(w2[n][0:HALF], a["w2"][e].rearrange("p (j n) -> p j n", j=2)).then_inc(w_in[n], 16)
            for n in range(B):
                sp.wait_ge(w_in[n], 32 * (TILES // B))

        @block.gpsimd
        def _(pool):
            with pool.Fori(0, TURNS) as i:
                steps = 0

                def held(semaphore, value):
                    nonlocal steps
                    pool.wait_ge(semaphore, value)
                    pool.wait_ge(stepped, i * (UN // B * (B + 1)) + steps)
                    pool.tensor_tensor(spare[:], ident[:, 0:1], ident[:, 1:2], ALU.add).then_inc(stepped, 1)
                    steps += 1

                for b in range(UN):
                    n, half = b % B, b // B
                    held(turned[n], nth(i, b))
                    if n == 0:
                        pool.tensor_copy(idx[half][:], tok_i[:, bass.ds(i * UN + b, B)]).then_inc(idx_in, 1)
                        held(idx_in, i * (UN // B) + (half + 1))
                    pool.indirect_dma_start(rows[n][:], None, a["x_rows"], bass.IndirectOffsetOnAxis(
                        ap=idx[half][:, n:n + 1], axis=0)).then_inc(rows_in[n], 16)
            for n in range(B):
                pool.wait_ge(rows_in[n], 16 * (TILES // B))

        @block.tensor
        def _(pe):
            pe.wait_ge(padded, B + 2)
            with pe.Fori(0, TURNS) as i:
                def turn(b):
                    n = b % B
                    pe.wait_ge(rows_in[n], 16 * nth(i, b) + 16)
                    pe.wait_ge(xt_in, i * UN + max(0, b - 1))
                    for k in range(KT):
                        mm = pe.transpose(xt_ps[b % 2][:, k * P:(k + 1) * P], rows[n][:, k * P:(k + 1) * P], ident[:])
                    mm.then_inc(turned[n], 1)

                def up(b):
                    n = b % B
                    pe.wait_ge(w_in[n], 32 * nth(i, b) + 32)
                    pe.wait_ge(xt_in, i * UN + (b + 1))
                    pe.wait_ge(h_in, i * UN + max(0, b - 1))
                    for j in range(2):
                        for k in range(KT):
                            mm = pe.matmul(h_ps[b % 2][0:HALF, j * P:(j + 1) * P], w1[n][:, k, j], xt[b % 2][:, k],
                                           start=(k == 0), stop=(k == KT - 1))
                    mm.then_inc(h_made, 1)

                def down(b):
                    n = b % B
                    pe.wait_ge(h_in, i * UN + (b + 1))
                    pe.wait_ge(y_in, i * UN + max(0, b - 1))
                    for j in range(2):
                        mm = pe.matmul(y_ps[b % 2][:, 0:E], ht[b % 2][:, j], w2[n][:, j], start=(j == 0), stop=(j == 1))
                    mm.then_inc(y_made[n], 1)

                turn(0)
                for b in range(UN + 1):
                    if b + 1 < UN:
                        turn(b + 1)
                    if b < UN:
                        up(b)
                    if b >= 1:
                        down(b - 1)

        @block.scalar
        def _(act):
            act.wait_ge(padded, 2 + B)
            with act.Fori(0, TURNS) as i:
                def silu_tile(b):
                    act.wait_ge(h_made, i * UN + (b + 1))
                    act.wait_ge(y_in, i * UN + max(0, b - 1))
                    act.activation(ht[b % 2][0:HALF], h_ps[b % 2][0:HALF, 0:2 * P].rearrange(
                        "p (j t) -> p j t", j=2), ACT.Silu).then_inc(h_in, 1)

                def write(b):
                    act.wait_ge(y_in, i * UN + (b + 1))
                    at = a["y_rows"].rearrange("(t p) n -> t p n", p=P)[i * UN + b]
                    act.dma_start(at, y_sb[b % B][:]).then_inc(y_out[b % B], 16)

                for b in range(UN):
                    act.wait_ge(turned[b % B], nth(i, b) + 1)
                    act.wait_ge(h_made, i * UN + max(0, b - 1))
                    act.activation(xt[b % 2][:], xt_ps[b % 2][:, 0:KT * P].rearrange("p (k t) -> p k t", k=KT),
                                   ACT.Copy).then_inc(xt_in, 1)
                    if b >= 1:
                        silu_tile(b - 1)
                    if b >= 3:
                        write(b - 3)
                silu_tile(UN - 1)
                for b in range(UN - 3, UN):
                    write(b)

            for n in range(B):
                act.wait_ge(y_out[n], 16 * (TILES // B))

        @block.vector
        def _(dve):
            for m in w2:
                dve.memset(m[:], 0.0).then_inc(padded, 1)
            for m in ht:
                dve.memset(m[:], 0.0).then_inc(padded, 1)

            with dve.Fori(0, TURNS) as i:
                for b in range(UN):
                    n = b % B
                    dve.wait_ge(y_made[n], nth(i, b) + 1)
                    dve.wait_ge(y_out[n], 16 * nth(i, b))
                    dve.tensor_copy(y_sb[n][:], y_ps[b % 2][:, 0:E]).then_inc(y_in, 1)


def combine(nc, a, keep):
    with ExitStack() as ctx:
        sb, ps, sem = scope(nc, ctx, "comb")
        x, weight, slot_i = keep["x"], keep["weight"], keep["slot_i"]
        norm = norm_parts((sb, ps, sem), keep, turn=False)
        B = 12
        got = [sb(f"got{i}", [P, E]) for i in range(B)]
        got_in = [sem(f"got_in{i}") for i in range(B)]
        added = sem("added")
        stored = sem("stored")
        block = ctx.enter_context(nc.Block())

        @block.gpsimd
        def _(pool):
            for c in range(NCH):
                for n in range(c * TC * TOP, (c + 1) * TC * TOP):
                    t, k = divmod(n, TOP)
                    if n >= B:
                        t0, k0 = divmod(n - B, TOP)
                        if k0 == TOP - 1:
                            pool.wait_ge(norm["summed"], t0 + 1)
                        else:
                            pool.wait_ge(added, t0 * (TOP - 1) + k0 + 1)
                    pool.indirect_dma_start(got[n % B][:], None, a["y_rows"], bass.IndirectOffsetOnAxis(
                        ap=slot_i[:, t, k:k + 1], axis=0)).then_inc(got_in[n % B], 16)
                if c >= 1:
                    norm_root(pool, norm, c - 1)
            norm_root(pool, norm, NCH - 1)

        @block.vector
        def _(dve):
            def gather(c):
                for t in range(c * TC, (c + 1) * TC):
                    for k in range(TOP):
                        n = t * TOP + k
                        dve.wait_ge(got_in[n % B], 16 * (n // B + 1))
                        if k:
                            dve.wait_ge(added, t * (TOP - 1) + k)
                        op = dve.scalar_tensor_tensor(x[:, t], got[n % B][:], weight[:, t, k:k + 1], x[:, t],
                                                      ALU.mult, ALU.add)
                        op.then_inc(added if k < TOP - 1 else norm["summed"], 1)
            for c in range(NCH):
                gather(c)
                norm_measure(dve, norm, c)
                if c >= 1:
                    norm_scale(dve, norm, c - 1)
            norm_scale(dve, norm, NCH - 1)

        @block.sync
        def _(sp):
            for c in range(NCH):
                sp.wait_ge(norm["normed"], (c + 1) * TC)
                sp.dma_start(a["out"].rearrange("(t p) n -> p t n", p=P)[:, c * TC:(c + 1) * TC],
                             x[:, c * TC:(c + 1) * TC]).then_inc(stored, 16)
            sp.wait_ge(stored, 16 * NCH)


def moe(nc, a, keep):
    with ExitStack() as ctx:
        sb, ps, sem = scope(nc, ctx, "moe")
        keep = dict(keep, weight=sb("weight", [P, NT, TOP]), slot_i=sb("slot_i", [P, NT, TOP], I32),
                    tok_i=sb("tok_i", [P, TILES], I32), owner=sb("owner", [1, 2 * P], I32))
        with ExitStack() as own:
            keep["y_sh"] = scope(nc, own, "moe")[0]("y_sh", [P, NT, E])
            route(nc, a, keep)
        experts(nc, a, keep)
        combine(nc, a, keep)


def program(nc, a, out, stages=9):
    with ExitStack() as ctx:
        sb, ps, sem = scope(nc, ctx, "keep")
        keep = dict(x=sb("x", [P, NT, E]), x_t=sb("x_t", [P, KT, TOK]), ident=sb("ident", [P, P]),
                    ident_bf=sb("ident_bf", [P, P], BF16), neg_half=sb("neg_half", [P, NT]))
        if stages >= 0:
            with ExitStack() as own:
                sb0 = scope(nc, own, "l0")[0]
                keep.update(v_all=sb0("v_all", [P, 2 * BATCH + 1, KTS, P]),
                            o_tok=sb0("o_tok", [P, 2 * BATCH, KTS, P]),
                            q_st=[sb0(f"q_st{i}", [P, QC, G0, CH], BF16) for i in range(2)],
                            k_st=[sb0(f"k_st{i}", [P, G0, SEQ], BF16) for i in range(2)],
                            v_st=[sb0(f"v_st{i}", [P, KTS, G0, 2 * D0]) for i in range(2)])
                project_qkv(nc, a, keep)
                attention(nc, a, keep)
                project_out(nc, a, keep)
        if stages >= 2:
            quantised_ffn(nc, a, keep)
        if stages >= 3:
            retention(nc, a, keep)
        if stages >= 4:
            moe(nc, dict(a, out=out), keep)
        else:
            store(nc, a, keep, out)


def store(nc, a, keep, out):
    with ExitStack() as ctx:
        sb, ps, sem = scope(nc, ctx, "store")
        stored = sem("stored")
        block = ctx.enter_context(nc.Block())

        @block.sync
        def _(sp):
            for c in range(NCH):
                sp.dma_start(out.rearrange("(t p) n -> p t n", p=P)[:, c * TC:(c + 1) * TC],
                             keep["x"][:, c * TC:(c + 1) * TC]).then_inc(stored, 16)
            sp.wait_ge(stored, 16 * NCH)


def lay_out(i):
    import numpy as np
    t = lambda w: np.ascontiguousarray(np.swapaxes(w, -1, -2))
    d = {}
    x = np.asarray(i["L0_attn_x"]).reshape(TOK, E)
    d["x"], d["x_t"] = x, t(x)
    w = np.asarray(i["L0_attn_w_qkv"])
    d["w_qk"], d["w_v"] = t(w[:2 * E]), t(w[2 * E:])
    d["w_out"], d["b_out"] = t(np.asarray(i["L0_attn_w_out"])), np.asarray(i["L0_attn_b_out"])
    for k in ("w_gate", "w_up", "w_down"):
        d[k] = np.asarray(i["L0_ffn_" + k]).view(np.int32)
    for k in ("s_gate", "s_up"):
        d[k] = t(np.asarray(i["L0_ffn_" + k]).reshape(MT, P))
    d["s_down"] = np.asarray(i["L0_ffn_s_down"])
    w = np.asarray(i["L1_attn_wqkv"]).reshape(H1, 3, D1, E)
    for n, k in enumerate(("w_q1", "w_k1", "w_v1")):
        d[k] = t(w[:, n].reshape(E, E))
    d["w_g1"], d["w_o1"] = t(np.asarray(i["L1_attn_wg"])), t(np.asarray(i["L1_attn_wo"]))
    d["gn_w"], d["gn_b"] = (t(np.repeat(np.asarray(i["L1_attn_gn_" + k]), D1).reshape(KT, P))
                            for k in ("weight", "bias"))
    d["tables"] = retention_tables()
    d["w_router"] = t(np.asarray(i["L1_ffn_gate_w"]))
    w1, w2 = t(np.asarray(i["L1_ffn_experts_w1"])), t(np.asarray(i["L1_ffn_experts_w2"]))
    rows = lambda w, k: np.ascontiguousarray(w.reshape(EXPERTS, k, w.shape[1] // k, w.shape[2]).transpose(
        0, 2, 1, 3).reshape(EXPERTS, w.shape[1] // k, k * w.shape[2]))
    d["w1"], d["w2"] = rows(w1, KT), rows(w2, 2)
    d["w_sh_up"], d["w_sh_down"] = t(np.asarray(i["L1_ffn_shared_gate_up"])), t(np.asarray(i["L1_ffn_shared_down"]))
    return d


def kernel(**inputs):
    import concourse.bacc as bacc
    from concourse.bass_utils import run_bass_kernel_spmd

    nc = bacc.Bacc("TRN2", target_bir_lowering=False, num_devices=1)
    arrays, a = {}, {}
    for name, v in lay_out(inputs).items():
        arrays[f"in_{name}"] = v
        a[name] = nc.dram_tensor(f"in_{name}", v.shape, mybir.dt.from_np(v.dtype), kind="ExternalInput").ap()
    scratch(nc, a)
    out = nc.dram_tensor("out_0", (TOK, E), F32, kind="ExternalOutput").ap()
    program(nc, a, out)
    r = run_bass_kernel_spmd(nc, [arrays], core_ids=[0])
    return r.results[0]["out_0"].reshape(BATCH, SEQ, E)


def scratch(nc, a):
    a["parts"] = nc.dram_tensor("parts", (GROUPS + 1, 2, PARTS, G0 * D0, SEQ), BF16, kind="Internal").ap()
    a["x_rows"] = nc.dram_tensor("x_rows", (TOK, E), F32, kind="Internal").ap()
    a["owners"] = nc.dram_tensor("owners", (2 * P,), I32, kind="Internal").ap()
    a["y_rows"] = nc.dram_tensor("y_rows", (TILES * P, E), F32, kind="Internal").ap()
```

```python
from contextlib import ExitStack

import concourse.bass as bass
from concourse import mybir

F32 = mybir.dt.float32
BF16 = mybir.dt.bfloat16
I8 = mybir.dt.int8
I32 = mybir.dt.int32
U32 = mybir.dt.uint32
ALU = mybir.AluOpType
ACT = mybir.ActivationFunctionType
AX = mybir.AxisListType

P = 128
BATCH, SEQ, E = 2, 1024, 256
TOK = BATCH * SEQ
KT = E // P
NT = TOK // P
CH = 512
NCH = TOK // CH
EPS = 1e-5
CREDIT = 1

H0, D0 = 16, 16
G0 = 4
GROUPS = BATCH * H0 // G0
KTS = SEQ // P
QC = SEQ // CH
PARTS = 3
PAIRS = ((0, 0), (0, 1), (1, 0), (1, 1), (0, 2), (2, 0))
STACK = len(PAIRS) * D0
ROWS = STACK + PARTS
SCALE0 = float(D0) ** -0.5


def scope(nc, ctx, tag):
    made = []

    def sb(name, shape, dt=F32):
        return ctx.enter_context(nc.sbuf_tensor(f"{tag}_{name}", shape, dt))

    def ps(name, shape=(P, CH), dt=F32):
        return ctx.enter_context(nc.psum_tensor(f"{tag}_{name}", list(shape), dt))

    def sem(name):
        made.append(nc.alloc_semaphore(f"{tag}_{name}"))
        return made[-1]

    def clear():
        if made:
            nc.clear_and_free_semaphores(made)
            nc.all_engine_barrier()

    ctx.callback(clear)
    return sb, ps, sem


def project_qkv(nc, a, keep):
    with ExitStack() as ctx:
        sb, ps, sem = scope(nc, ctx, "proj")
        w_qk = sb("w_qk", [P, KT, 2 * E])
        w_v = sb("w_v", [P, KT, E])
        x_t = keep["x_t"]
        SLOTS = 4
        parts = sb("parts", [P, SLOTS, PARTS, CH], BF16)
        rest = sb("rest", [P, 2, CH])
        qk_ps = [ps(f"qk{i}") for i in range(3)]
        v_ps = [ps(f"v{i}") for i in range(2)]
        loaded = [sem(f"loaded{c}") for c in range(NCH)]
        weights = sem("weights")
        v_weights = sem("v_weights")
        projected, high_done, rest_done, mid_done, low_done = (sem(n) for n in (
            "projected", "high_done", "rest_done", "mid_done", "low_done"))
        saved = [sem(f"saved{i}") for i in range(SLOTS)]
        v_done, v_kept = sem("v_done"), sem("v_kept")
        cleared = sem("cleared")
        v_all, ident, ident_bf = keep["v_all"], keep["ident"], keep["ident_bf"]
        x, bias = keep["x"], sb("bias", [P, E])
        x_in, biased = sem("x_in"), sem("biased")
        blocks = [(c, m) for c in range(NCH) for m in range(4)]
        writes = {n: 0 for n in range(len(blocks))}
        done_by = []
        count = [0] * SLOTS
        for n, (c, m) in enumerate(blocks):
            k = 3 if (c < QC and m % 2 == 0) else 2
            count[n % SLOTS] += 16 * k
            done_by.append(count[n % SLOTS])

        block = ctx.enter_context(nc.Block())

        @block.sync
        def _(sp):
            sp.dma_start(w_qk[:], a["w_qk"].rearrange("(k p) n -> p k n", p=P)).then_inc(weights, 16)
            for c in range(NCH):
                sp.dma_start(x_t[:, :, c * CH:(c + 1) * CH],
                             a["x_t"].rearrange("(k p) n -> p k n", p=P)[:, :, c * CH:(c + 1) * CH]
                             ).then_inc(loaded[c], 16)
            sp.dma_start(x[:], a["x"].rearrange("(t p) n -> p t n", p=P)).then_inc(x_in, 16)
            sp.dma_start(bias[:], a["b_out"].partition_broadcast(P)).then_inc(x_in, 16)
            for n, (c, m) in enumerate(blocks):
                sp.wait_ge(low_done, n + 1)
                qk, half, b, cc = m // 2, m % 2, c // QC, c % QC
                for p in range(2):
                    group = 2 * (2 * b + half) + p
                    for g in ([group, GROUPS] if group == 0 else [group]):
                        sp.dma_start(a["parts"][g, qk, :, :, cc * CH:(cc + 1) * CH].rearrange("a r t -> r a t"),
                                     parts[64 * p:64 * p + 64, n % SLOTS]).then_inc(saved[n % SLOTS], 16)
            for slot in range(SLOTS):
                sp.wait_ge(saved[slot], count[slot])

        @block.gpsimd
        def _(pool):
            done = 0

            def ordered(instruction):
                nonlocal done
                instruction.then_inc(cleared, 1)
                done += 1
                pool.wait_ge(cleared, done)

            for m in (ident, ident_bf):
                ordered(pool.memset(m[:], 0.0))
                ordered(pool.affine_select(out=m[:], in_=m[:], compare_op=ALU.not_equal, fill=1.0,
                                           base=0, pattern=[[-1, P]], channel_multiplier=1))
            ordered(pool.memset(v_all[:, 2 * BATCH], 0.0))
            ordered(pool.memset(keep["neg_half"][:], -0.5))
            for buf in range(2):
                ordered(pool.memset(keep["v_st"][buf][:], 1.0))
                rows = keep["k_st"][buf][STACK:P].rearrange("r h (j k) -> r h j k", k=P)
                ordered(pool.memset(rows, 0.0))
                for part in range(PARTS):
                    ordered(pool.affine_select(out=rows, in_=rows, compare_op=ALU.not_equal, fill=1.0,
                                               base=-KTS * part, pattern=[[0, G0], [-1, KTS], [0, P]],
                                               channel_multiplier=1))
            pool.wait_ge(x_in, 32)
            for t in range(NT):
                pool.tensor_tensor(x[:, t], x[:, t], bias[:], ALU.add).then_inc(biased, 1)

        @block.tensor
        def _(pe):
            pe.wait_ge(weights, 16)
            for n, (c, m) in enumerate(blocks):
                if m == 0:
                    pe.wait_ge(loaded[c], 16)
                if n >= 3:
                    pe.wait_ge(rest_done, n - 2)
                for k in range(KT):
                    mm = pe.matmul(qk_ps[n % 3][:], w_qk[:, k, m * P:(m + 1) * P],
                                   x_t[:, k, c * CH:(c + 1) * CH], start=(k == 0), stop=(k == KT - 1))
                mm.then_inc(projected, 1)
            pe.wait_ge(v_weights, 16)
            for t in range(NT):
                if t >= 2:
                    pe.wait_ge(v_kept, t - 1)
                for k in range(KT):
                    mm = pe.matmul(v_ps[t % 2][:, 0:E], x_t[:, k, t * P:(t + 1) * P], w_v[:, k, :],
                                   start=(k == 0), stop=(k == KT - 1))
                mm.then_inc(v_done, 1)

        @block.scalar
        def _(act):
            act.dma_start(w_v[:], a["w_v"].rearrange("(k p) n -> p k n", p=P)).then_inc(v_weights, 16)
            for n in range(len(blocks)):
                act.wait_ge(projected, n + 1)
                if n >= SLOTS:
                    act.wait_ge(saved[n % SLOTS], done_by[n - SLOTS])
                act.activation(parts[:, n % SLOTS, 0], qk_ps[n % 3][:], ACT.Copy).then_inc(high_done, 1)
            for t in range(NT):
                act.wait_ge(v_done, t + 1)
                b, kt = t // KTS, t % KTS
                act.activation(v_all[:, 2 * b:2 * b + 2, kt, :],
                               v_ps[t % 2][:, 0:E].rearrange("p (j n) -> p j n", j=2), ACT.Copy).then_inc(v_kept, 1)

        @block.vector
        def _(dve):
            for n in range(len(blocks)):
                dve.wait_ge(high_done, n + 1)
                dve.tensor_tensor(rest[:, n % 2], qk_ps[n % 3][:], parts[:, n % SLOTS, 0],
                                  ALU.subtract).then_inc(rest_done, 1)
                dve.wait_ge(rest_done, n + 1)
                dve.tensor_copy(parts[:, n % SLOTS, 1], rest[:, n % 2]).then_inc(mid_done, 1)
                dve.wait_ge(mid_done, n + 1)
                dve.tensor_tensor(parts[:, n % SLOTS, 2], rest[:, n % 2], parts[:, n % SLOTS, 1],
                                  ALU.subtract).then_inc(low_done, 1)


def attention(nc, a, keep):
    with ExitStack() as ctx:
        sb, ps, sem = scope(nc, ctx, "attn")
        v_all, ident, ident_bf, o_tok = keep["v_all"], keep["ident"], keep["ident_bf"], keep["o_tok"]
        q_st, k_st, v_st = keep["q_st"], keep["k_st"], keep["v_st"]
        QT = CH // P
        NB = G0 * QT
        probs = [sb(f"probs{i}", [P, G0, CH]) for i in range(2)]
        pv_sb = [sb(f"pv_sb{i}", [P, CH]) for i in range(2)]
        neg = sb("neg", [P, NB, KTS])
        neg_rest = sb("neg_rest", [P, NB, KTS])
        neg_least = sb("neg_least", [P, NB])
        neg_parts = sb("neg_parts", [P, NB, 32], BF16)
        gap = sb("gap", [P, NB, KTS])
        wj = [sb(f"wj{i}", [P, NB, KTS]) for i in range(2)]
        pv_t = [sb(f"pv_t{i}", [P, KTS, NB, D0 + 1]) for i in range(2)]
        coef = [sb(f"coef{i}", [P, NB, KTS]) for i in range(2)]
        total = sb("total", [P, NB])
        prod = sb("prod", [P, KTS, NB, D0])
        st_ps = [ps(f"st{h}") for h in range(G0)]
        mx_ps = [ps(f"mx{i}") for i in range(2)]
        o_ps = ps("o")
        turn_ps = ps("turn")

        stack = [sem(f"stack{i}") for i in range(2)]
        v_staged = sem("v_staged")
        scored, maxed = sem("scored"), sem("maxed")
        neg_chain, neg_split = sem("neg_chain"), sem("neg_split")
        neg_turned, neg_kept = sem("neg_turned"), sem("neg_kept")
        gap_in, wj_in = sem("gap_in"), sem("wj_in")
        st_made, exp_done, pv_done = sem("st_made"), sem("exp_done"), sem("pv_done")
        pv_copied, pv_turned, pv_kept = sem("pv_copied"), sem("pv_turned"), sem("pv_kept")
        coef_chain, coef_in, combine_chain, combined = (sem(n) for n in (
            "coef_chain", "coef_in", "combine_chain", "combined"))
        padded = sem("padded")

        UNITS = 2 * QC
        STEPS = UNITS * KTS
        SM = NB * 2
        TURNS = GROUPS // 2
        LOADS = (1 + QC) * len(PAIRS)
        DEAL = [4, 4, 4, 5, 5, 5, 5, 0]
        SPREAD = {0: (0, 0, 0, 0, 0, 0), 4: (0, 1, 0, 1, 1, 1), 5: (1, 0, 1, 1, 1, 1)}

        block = ctx.enter_context(nc.Block())

        @block.sync
        def _(sp):
            def load_stack(buf, g):
                for j, (qp, kp) in enumerate(PAIRS):
                    rows = slice(D0 * j, D0 * j + D0)
                    q_part = a["parts"][g, 0, qp].rearrange("(h d) t -> d h t", d=D0)
                    k_part = a["parts"][g, 1, kp].rearrange("(h d) t -> d h t", d=D0)
                    sp.dma_start(k_st[buf][rows], k_part).then_inc(stack[buf], 16)
                    for c in range(QC):
                        sp.dma_start(q_st[buf][rows, c], q_part[:, :, c * CH:(c + 1) * CH]).then_inc(stack[buf], 16)

            load_stack(0, 0)
            with sp.Fori(0, TURNS) as i:
                sp.wait_ge(st_made, CREDIT + i * (STEPS * G0))
                load_stack(1, 2 * i + 1)
                sp.wait_ge(st_made, CREDIT + i * (STEPS * G0) + STEPS * G0 // 2)
                load_stack(0, 2 * i + 2)
            sp.wait_ge(stack[0], 16 * LOADS * (TURNS + 1))

        @block.gpsimd
        def _(pool):
            pool.sem_inc(combined, CREDIT)

            def stage_v(buf, i):
                pool.tensor_copy(v_st[buf][:, :, :, 0:D0],
                                 v_all[:, i, :, 64 * buf:64 * buf + 64].rearrange("p k (h d) -> p k h d", d=D0)
                                 ).then_inc(v_staged, 1)

            pool.memset(prod[:], 0.0).then_inc(combined, 1)
            pool.wait_ge(combined, CREDIT + 1)
            stage_v(0, 0)
            with pool.Fori(0, TURNS) as i:
                def combine(w):
                    u = i * UNITS + w
                    pool.wait_ge(coef_in, u + 1)
                    pool.tensor_tensor(prod[:], pv_t[w % 2][:, :, :, 0:D0],
                                       coef[w % 2][:].rearrange("p n k -> p k n").unsqueeze(3)
                                       .to_broadcast([P, KTS, NB, D0]), ALU.mult).then_inc(combine_chain, 1)
                    pool.wait_ge(combine_chain, i * (3 * UNITS) + 3 * w + 1)
                    pool.tensor_tensor(prod[:, 0:4], prod[:, 0:4], prod[:, 4:8], ALU.add).then_inc(combine_chain, 1)
                    pool.wait_ge(combine_chain, i * (3 * UNITS) + 3 * w + 2)
                    pool.tensor_tensor(prod[:, 0:2], prod[:, 0:2], prod[:, 2:4], ALU.add).then_inc(combine_chain, 1)
                    pool.wait_ge(combine_chain, i * (3 * UNITS) + 3 * w + 3)
                    c, p = w % 2, w // 2
                    out = o_tok[:, i, c * QT:(c + 1) * QT, 64 * p:64 * p + 64].rearrange("p q (h d) -> p h q d", d=D0)
                    pool.tensor_tensor(out, prod[:, 0].rearrange("p (h q) d -> p h q d", h=G0),
                                       prod[:, 1].rearrange("p (h q) d -> p h q d", h=G0),
                                       ALU.add).then_inc(combined, 1)
                    pool.wait_ge(combined, CREDIT + u + 2)

                pool.wait_ge(pv_done, CREDIT + i * STEPS)
                stage_v(1, i)
                combine(0)
                combine(1)
                pool.wait_ge(pv_done, CREDIT + i * STEPS + STEPS // 2)
                stage_v(0, i + 1)
                combine(2)
                combine(3)

        @block.tensor
        def _(pe):
            for semaphore in (st_made, pv_done, pv_turned):
                pe.sem_inc(semaphore, CREDIT)

            def score_rows(buf, c, n):
                h, qt, half = n // (2 * QT), n // 2 % QT, n % 2
                pe.matmul(mx_ps[n % 2][:], q_st[buf][0:STACK, c, h, qt * P:(qt + 1) * P],
                          k_st[buf][0:STACK, h, half * CH:(half + 1) * CH],
                          start=True, stop=True).then_inc(scored, 1)

            def turn_neg(unit):
                pe.wait_ge(neg_split, unit + 1)
                for r in range(2):
                    for n in range(NB // 2):
                        mm = pe.transpose(mx_ps[r][:].bitcast(BF16)[96:P, n * P:(n + 1) * P],
                                          neg_parts[:, r * (NB // 2) + n], ident_bf[:])
                    mm.then_inc(neg_turned, 1)

            pe.wait_ge(stack[0], 16 * LOADS)
            for n in range(SM):
                if n >= 2:
                    pe.wait_ge(maxed, n - 1)
                score_rows(0, 0, n)
            turn_neg(0)
            with pe.Fori(0, TURNS) as i:
                def score_next(w, n):
                    pe.wait_ge(maxed, i * (UNITS * SM) + (SM * (w + 1) + n - 1))
                    score_rows(((w + 1) // 2) % 2, (w + 1) % 2, n)

                def pv(step):
                    w, kt = step // KTS, step % KTS
                    pe.wait_ge(pv_copied, CREDIT + i * STEPS + step)
                    if kt == 0 and w % 2 == 0:
                        pe.wait_ge(v_staged, 2 * i + (w // 2 + 1))
                    for h in range(G0):
                        pe.wait_ge(exp_done, CREDIT + i * (STEPS * G0) + (step * G0 + h + 1))
                        mm = pe.matmul(o_ps[32 * h:32 * h + 32, :], v_st[w // 2][:, kt, h], probs[step % 2][:, h],
                                       start=True, stop=True)
                    mm.then_inc(pv_done, 1)

                def turn_pv(step):
                    pe.wait_ge(pv_copied, CREDIT + i * STEPS + (step + 1))
                    pe.wait_ge(pv_kept, CREDIT + i * STEPS + step)
                    for qt in range(QT):
                        mm = pe.transpose(turn_ps[:, qt * P:(qt + 1) * P], pv_sb[step % 2][:, qt * P:(qt + 1) * P],
                                          ident[:])
                    mm.then_inc(pv_turned, 1)

                for w in range(UNITS):
                    buf, c = w // 2, w % 2
                    nbuf = ((w + 1) // 2) % 2
                    pe.wait_ge(neg_kept, i * (2 * UNITS) + 2 * (w + 1))
                    if w % 2 == 1:
                        pe.wait_ge(stack[nbuf], i * (16 * LOADS) + 16 * LOADS * (1 if nbuf else 2))
                    n = 0
                    for kt in range(KTS):
                        step = w * KTS + kt
                        spread = SPREAD[DEAL[kt]]
                        for h in range(G0):
                            pe.wait_ge(exp_done, CREDIT + i * (STEPS * G0) + ((step - 1) * G0 + h + 1 if step else 0))
                            pe.matmul(st_ps[h][:], k_st[buf][:, h, kt * P:(kt + 1) * P], q_st[buf][:, c, h],
                                      start=True, stop=True).then_inc(st_made, 1)
                            for _ in range(spread[h]):
                                score_next(w, n)
                                n += 1
                        if step >= 1:
                            pv(step - 1)
                        if kt == KTS - 1:
                            turn_neg(i * UNITS + w + 1)
                        for _ in range(spread[G0]):
                            score_next(w, n)
                            n += 1
                        if step >= 2:
                            turn_pv(step - 2)
                        for _ in range(spread[G0 + 1]):
                            score_next(w, n)
                            n += 1
                pv(STEPS - 1)
                turn_pv(STEPS - 2)
                turn_pv(STEPS - 1)

        @block.scalar
        def _(act):
            for semaphore in (exp_done, pv_copied, pv_kept):
                act.sem_inc(semaphore, CREDIT)

            def copy_pv(i, step):
                act.wait_ge(pv_done, CREDIT + i * STEPS + (step + 1))
                act.wait_ge(pv_turned, CREDIT + i * STEPS + max(0, step - 1))
                act.activation(pv_sb[step % 2][:], o_ps[:], ACT.Copy).then_inc(pv_copied, 1)

            def keep_pv(i, step):
                w, kt = step // KTS, step % KTS
                if kt == 0:
                    act.wait_ge(combined, CREDIT + i * UNITS + w)
                act.wait_ge(pv_turned, CREDIT + i * STEPS + (step + 1))
                act.activation(pv_t[w % 2][:, kt].rearrange("p (h q) d -> p q h d", h=G0),
                                turn_ps[:].rearrange("p (q h d) -> p q h d", q=QT, h=G0)[:, :, :, 0:D0 + 1], ACT.Copy
                                ).then_inc(pv_kept, 1)

            act.wait_ge(gap_in, 1)
            act.activation(wj[0][:], gap[:], ACT.Exp, scale=SCALE0).then_inc(wj_in, 1)
            with act.Fori(0, TURNS) as i:
                for w in range(UNITS):
                    for kt in range(KTS):
                        step = w * KTS + kt
                        act.wait_ge(pv_done, CREDIT + i * STEPS + max(0, step - 1))
                        for h in range(G0):
                            act.wait_ge(st_made, CREDIT + i * (STEPS * G0) + (step * G0 + h + 1))
                            act.activation(probs[step % 2][:, h], st_ps[h][:], ACT.Exp,
                                           scale=SCALE0).then_inc(exp_done, 1)
                        if step >= 1:
                            copy_pv(i, step - 1)
                        if step >= 2:
                            keep_pv(i, step - 2)
                    if w < UNITS - 1:
                        act.wait_ge(gap_in, i * UNITS + (w + 2))
                        act.wait_ge(combined, CREDIT + i * UNITS + (w + 1))
                        act.activation(wj[(w + 1) % 2][:], gap[:], ACT.Exp, scale=SCALE0).then_inc(wj_in, 1)
                copy_pv(i, STEPS - 1)
                keep_pv(i, STEPS - 2)
                keep_pv(i, STEPS - 1)
                act.wait_ge(gap_in, i * UNITS + (UNITS + 1))
                act.wait_ge(combined, CREDIT + i * UNITS + UNITS)
                act.activation(wj[0][:], gap[:], ACT.Exp, scale=SCALE0).then_inc(wj_in, 1)

        @block.vector
        def _(dve):
            def reduce(n, made):
                dve.wait_ge(scored, made)
                dve.tensor_reduce(neg[:, n // 2, n % 2 * QT:n % 2 * QT + QT],
                                  mx_ps[n % 2][:].rearrange("p (j k) -> p j k", k=P), AX.X,
                                  ALU.max, negate=True).then_inc(maxed, 1)

            def split_neg(unit):
                part = [neg_parts[:, :, j * KTS:(j + 1) * KTS] for j in range(PARTS)]
                dve.wait_ge(maxed, unit * SM + SM)
                dve.wait_ge(wj_in, unit)
                dve.tensor_copy(part[0], neg[:]).then_inc(neg_chain, 1)
                dve.tensor_reduce(neg_least[:], neg[:], AX.X, ALU.min).then_inc(neg_chain, 1)
                dve.wait_ge(neg_chain, unit * 4 + 1)
                dve.tensor_tensor(neg_rest[:], neg[:], part[0], ALU.subtract).then_inc(neg_chain, 1)
                dve.wait_ge(neg_chain, unit * 4 + 3)
                dve.tensor_copy(part[1], neg_rest[:]).then_inc(neg_chain, 1)
                dve.wait_ge(neg_chain, unit * 4 + 4)
                dve.tensor_tensor(part[2], neg_rest[:], part[1], ALU.subtract).then_inc(neg_split, 1)
                dve.tensor_tensor(gap[:], neg_least[:].unsqueeze(2).to_broadcast([P, NB, KTS]), neg[:],
                                  ALU.subtract).then_inc(gap_in, 1)

            def keep_neg(unit, buf, c):
                for r in range(2):
                    dve.wait_ge(neg_turned, unit * 2 + r + 1)
                    dve.tensor_copy(q_st[buf][96:P, c, 2 * r:2 * r + 2],
                                    mx_ps[r][:].bitcast(BF16)[96:P, :].rearrange("p (h t) -> p h t", h=2)
                                    ).then_inc(neg_kept, 1)

            def coefficients(i, w):
                u = i * UNITS + w
                c0 = i * (3 * UNITS) + 3 * w
                dve.wait_ge(pv_kept, CREDIT + i * STEPS + (w + 1) * KTS)
                dve.wait_ge(wj_in, u + 1)
                dve.tensor_tensor(coef[w % 2][:], wj[w % 2][:], pv_t[w % 2][:, :, :, D0].rearrange("p k n -> p n k"),
                                  ALU.mult).then_inc(coef_chain, 1)
                dve.wait_ge(coef_chain, c0 + 1)
                dve.tensor_reduce(total[:], coef[w % 2][:], AX.X, ALU.add).then_inc(coef_chain, 1)
                dve.wait_ge(coef_chain, c0 + 2)
                dve.reciprocal(total[:], total[:]).then_inc(coef_chain, 1)
                dve.wait_ge(coef_chain, c0 + 3)
                dve.tensor_tensor(coef[w % 2][:], coef[w % 2][:], total[:].unsqueeze(2).to_broadcast([P, NB, KTS]),
                                  ALU.mult).then_inc(coef_in, 1)

            dve.memset(neg_parts[:], 0.0).then_inc(padded, 1)
            dve.wait_ge(padded, 1)
            for n in range(SM):
                reduce(n, n + 1)
            split_neg(0)
            keep_neg(0, 0, 0)
            with dve.Fori(0, TURNS) as i:
                for w in range(UNITS):
                    n = 0
                    for kt in range(KTS):
                        step = w * KTS + kt
                        for m in range(DEAL[kt]):
                            if m == 2 and step >= KTS and kt == 2:
                                coefficients(i, w - 1)
                            reduce(n, i * (UNITS * SM) + (SM * (w + 1) + n + 1))
                            n += 1
                        if kt == KTS - 1:
                            keep_neg(i * UNITS + w + 1, ((w + 1) // 2) % 2, (w + 1) % 2)
                        if n == SM and DEAL[kt] and w < UNITS:
                            split_neg(i * UNITS + w + 1)
                coefficients(i, UNITS - 1)


INTER = 1024
MT = INTER // P
LAG = 1
TC = CH // P


def norm_parts(makers, keep, turn=True):
    sb, ps, sem = makers
    norm = dict(x=keep["x"], x_t=keep["x_t"], ident=keep["ident"], half=keep["neg_half"],
                turn_ps=[ps(f"turn{k}") for k in range(KT)] if turn else None,
                stats=sb("ln_stats", [P, NT, 6]), mv=sb("ln_mv", [P, NT, 2]),
                var=sb("ln_var", [P, NT]), rstd=sb("ln_rstd", [P, NT]))
    for name in ("summed", "stat", "aggr", "var_in", "rstd_in", "normed", "turned", "kept"):
        norm[name] = sem(name)
    return norm


def norm_add(dve, norm, t, y):
    x = norm["x"]
    return dve.tensor_tensor(x[:, t], y, x[:, t], ALU.add).then_inc(norm["summed"], 1)


def norm_measure(dve, norm, c):
    stats, mv = norm["stats"], norm["mv"]
    for t in range(c * TC, (c + 1) * TC):
        dve.wait_ge(norm["summed"], t + 1)
        dve.bn_stats(stats[:, t], norm["x"][:, t]).then_inc(norm["stat"], 1)
    for t in range(c * TC, (c + 1) * TC):
        dve.wait_ge(norm["stat"], t + 1)
        dve.bn_aggr(mv[:, t], stats[:, t]).then_inc(norm["aggr"], 1)
    dve.wait_ge(norm["aggr"], (c + 1) * TC)
    dve.tensor_scalar(norm["var"][:, c * TC:(c + 1) * TC], mv[:, c * TC:(c + 1) * TC, 1], EPS, None,
                      ALU.add).then_inc(norm["var_in"], 1)


def norm_root(pool, norm, c):
    pool.wait_ge(norm["var_in"], c + 1)
    pool.tensor_tensor(norm["rstd"][:, c * TC:(c + 1) * TC], norm["var"][:, c * TC:(c + 1) * TC],
                       norm["half"][:, 0:TC], ALU.pow).then_inc(norm["rstd_in"], 1)


def norm_scale(dve, norm, c):
    x, mv, rstd = norm["x"], norm["mv"], norm["rstd"]
    dve.wait_ge(norm["rstd_in"], c + 1)
    for t in range(c * TC, (c + 1) * TC):
        dve.tensor_scalar(x[:, t], x[:, t], mv[:, t, 0:1], rstd[:, t:t + 1],
                          ALU.subtract, ALU.mult).then_inc(norm["normed"], 1)


def norm_turn(pe, norm, c):
    if c:
        pe.wait_ge(norm["kept"], KT * c)
    for t in range(TC):
        pe.wait_ge(norm["normed"], c * TC + t + 1)
        for k in range(KT):
            mm = pe.transpose(norm["turn_ps"][k][:, t * P:(t + 1) * P],
                              norm["x"][:, c * TC + t, k * P:(k + 1) * P], norm["ident"][:])
    mm.then_inc(norm["turned"], 1)


def norm_keep(act, norm, c):
    act.wait_ge(norm["turned"], c + 1)
    for k in range(KT):
        act.activation(norm["x_t"][:, k, c * CH:(c + 1) * CH], norm["turn_ps"][k][:],
                       ACT.Copy).then_inc(norm["kept"], 1)


def project_out(nc, a, keep):
    with ExitStack() as ctx:
        sb, ps, sem = scope(nc, ctx, "out0")
        o_tok = keep["o_tok"]
        w = sb("w", [P, KT, E])
        o_t = [sb(f"o_t{i}", [P, KT, P]) for i in range(2)]
        y_ps = [ps(f"y{i}") for i in range(2)]
        o_ps = [ps(f"o{i}") for i in range(2)]
        w_up, w_down, s_up, s_down = (keep[n] for n in ("w_up", "w_down", "s_up", "s_down"))
        raw_up = sb("raw_up", [P, 2, KT, INTER], I8)
        raw_down = sb("raw_down", [P, MT, E], I8)
        weights, turned, turned_in, made = (sem(n) for n in ("weights", "o_turned", "o_turned_in", "made"))
        raw_in, scales, cast = (sem(n) for n in ("raw_in", "scales", "cast"))
        norm = norm_parts((sb, ps, sem), keep)
        block = ctx.enter_context(nc.Block())

        @block.sync
        def _(sp):
            sp.dma_start(w[:], a["w_out"].rearrange("(k p) n -> p k n", p=P)).then_inc(weights, 16)
            for j, name in enumerate(("w_gate", "w_up")):
                sp.dma_start(raw_up[:, j], a[name].bitcast(I8).rearrange("(k p) n -> p k n", p=P)).then_inc(raw_in, 16)
            sp.dma_start(raw_down[:], a["w_down"].bitcast(I8).rearrange("(k p) n -> p k n", p=P)).then_inc(raw_in, 16)
            for j, name in enumerate(("s_gate", "s_up")):
                sp.dma_start(s_up[:, j], a[name]).then_inc(scales, 16)
            sp.dma_start(s_down[:], a["s_down"].partition_broadcast(P)).then_inc(scales, 16)
            sp.wait_ge(scales, 48)

        @block.vector
        def _(dve):
            for c in range(NCH + LAG):
                if c < NCH:
                    for t in range(c * TC, (c + 1) * TC):
                        dve.wait_ge(made, t + 1)
                        norm_add(dve, norm, t, y_ps[t % 2][:, 0:E])
                    norm_measure(dve, norm, c)
                    norm_scale(dve, norm, c)

        @block.gpsimd
        def _(pool):
            for c in range(NCH):
                norm_root(pool, norm, c)
                if c == 0:
                    pool.wait_ge(raw_in, 48)
                    pool.tensor_copy(w_down[:], raw_down[:]).then_inc(cast, 1)

        @block.tensor
        def _(pe):
            def turn(t):
                b, tt = t // KTS, t % KTS
                if t >= 2:
                    pe.wait_ge(turned_in, t - 1)
                for k in range(KT):
                    mm = pe.transpose(o_ps[t % 2][:, k * P:(k + 1) * P], o_tok[:, 2 * b + k, tt], keep["ident"][:])
                mm.then_inc(turned, 1)

            turn(0)
            pe.wait_ge(weights, 16)
            for c in range(NCH + LAG):
                if c < NCH:
                    for t in range(c * TC, (c + 1) * TC):
                        if t + 1 < NT:
                            turn(t + 1)
                        pe.wait_ge(turned_in, t + 1)
                        if t >= 2:
                            pe.wait_ge(norm["summed"], t - 1)
                        for k in range(KT):
                            mm = pe.matmul(y_ps[t % 2][:, 0:E], o_t[t % 2][:, k], w[:, k],
                                           start=(k == 0), stop=(k == KT - 1))
                        mm.then_inc(made, 1)
                if c >= LAG:
                    norm_turn(pe, norm, c - LAG)

        @block.scalar
        def _(act):
            for c in range(NCH + LAG):
                if 1 <= c <= 2:
                    act.wait_ge(raw_in, 48)
                    act.activation(w_up[:, c - 1], raw_up[:, c - 1], ACT.Copy).then_inc(cast, 1)
                if c < NCH:
                    for t in range(c * TC, (c + 1) * TC):
                        act.wait_ge(turned, t + 1)
                        if t >= 2:
                            act.wait_ge(made, t - 1)
                        act.activation(o_t[t % 2][:], o_ps[t % 2][:, 0:KT * P].rearrange("p (k t) -> p k t", k=KT),
                                       ACT.Copy).then_inc(turned_in, 1)
                if c >= LAG:
                    norm_keep(act, norm, c - LAG)




def quantised_ffn(nc, a, keep):
    with ExitStack() as ctx:
        sb, ps, sem = scope(nc, ctx, "ffn0")
        x_t = keep["x_t"]
        w_up, w_down, s_up, s_down = (keep[n] for n in ("w_up", "w_down", "s_up", "s_down"))
        x_parts = [sb(f"x_parts{i}", [P, PARTS, KT, CH], BF16) for i in range(2)]
        x_rest = sb("x_rest", [P, KT, CH])
        gate = [sb(f"gate{i}", [P, CH]) for i in range(2)]
        fused = [sb(f"fused{i}", [P, MT, CH]) for i in range(2)]
        y_sb = [sb(f"y_sb{i}", [P, E]) for i in range(2)]
        g_ps = [ps(f"g{i}") for i in range(2)]
        u_ps = [ps(f"u{i}") for i in range(2)]
        y_ps = [ps(f"y{i}") for i in range(2)]
        split, halved = sem("split"), sem("halved")
        gated, upped, silu, fuse, made, scaled = (sem(n) for n in (
            "gated", "upped", "silu", "fuse", "made", "scaled"))
        norm = norm_parts((sb, ps, sem), keep)
        block = ctx.enter_context(nc.Block())

        @block.gpsimd
        def _(pool):
            for c in range(NCH):
                norm_root(pool, norm, c)

        @block.tensor
        def _(pe):
            def down(c):
                for t in range(TC):
                    n = c * TC + t
                    if n >= 2:
                        pe.wait_ge(scaled, n - 1)
                    for m in range(MT):
                        pe.wait_ge(fuse, c * MT + m + 1)
                        mm = pe.matmul(y_ps[n % 2][:, 0:E], fused[c % 2][:, m, t * P:(t + 1) * P], w_down[:, m],
                                       start=(m == 0), stop=(m == MT - 1))
                    mm.then_inc(made, 1)

            for c in range(NCH + 1):
                if c < NCH:
                    pe.wait_ge(split, 3 * c + 3)
                    for m in range(MT):
                        n = c * MT + m
                        for j, (bank, free, done) in enumerate(((g_ps, silu, gated), (u_ps, fuse, upped))):
                            if n >= 2:
                                pe.wait_ge(free, n - 1)
                            for k in range(KT):
                                for p in range(PARTS):
                                    mm = pe.matmul(bank[n % 2][:], w_up[:, j, k, m * P:(m + 1) * P],
                                                   x_parts[c % 2][:, p, k], start=(k == 0 and p == 0),
                                                   stop=(k == KT - 1 and p == PARTS - 1))
                            mm.then_inc(done, 1)
                if c >= 1:
                    down(c - 1)
                if c >= 2:
                    norm_turn(pe, norm, c - 2)
            norm_turn(pe, norm, NCH - 1)

        @block.scalar
        def _(act):
            for c in range(NCH + 2):
                if c < NCH:
                    for m in range(MT):
                        n = c * MT + m
                        act.wait_ge(gated, n + 1)
                        if n >= 2:
                            act.wait_ge(fuse, n - 1)
                        act.activation(gate[n % 2][:], g_ps[n % 2][:], ACT.Silu,
                                       scale=s_up[:, 0, m:m + 1]).then_inc(silu, 1)
                if c >= 2:
                    norm_keep(act, norm, c - 2)

        @block.vector
        def _(dve):
            def split_x(c):
                parts, chunk = x_parts[c % 2], x_t[:, :, c * CH:(c + 1) * CH]
                if c >= 2:
                    dve.wait_ge(upped, (c - 1) * MT)
                dve.tensor_copy(parts[:, 0], chunk).then_inc(split, 1)
                dve.wait_ge(split, 3 * c + 1)
                dve.tensor_tensor(x_rest[:], chunk, parts[:, 0], ALU.subtract).then_inc(halved, 1)
                dve.wait_ge(halved, c + 1)
                dve.tensor_copy(parts[:, 1], x_rest[:]).then_inc(split, 1)
                dve.wait_ge(split, 3 * c + 2)
                dve.tensor_tensor(parts[:, 2], x_rest[:], parts[:, 1], ALU.subtract).then_inc(split, 1)

            split_x(0)

            def close(c):
                for t in range(c * TC, (c + 1) * TC):
                    dve.wait_ge(made, t + 1)
                    if t >= 2:
                        dve.wait_ge(norm["summed"], t - 1)
                    dve.tensor_tensor(y_sb[t % 2][:], y_ps[t % 2][:, 0:E], s_down[:], ALU.mult).then_inc(scaled, 1)
                    dve.wait_ge(scaled, t + 1)
                    norm_add(dve, norm, t, y_sb[t % 2][:])
                norm_measure(dve, norm, c)
                norm_scale(dve, norm, c)

            for c in range(NCH + 1):
                if c < NCH:
                    for m in range(MT):
                        n = c * MT + m
                        if m == MT // 2 and c + 1 < NCH:
                            split_x(c + 1)
                        dve.wait_ge(upped, n + 1)
                        dve.wait_ge(silu, n + 1)
                        if c >= 2:
                            dve.wait_ge(made, (c - 1) * TC)
                        dve.scalar_tensor_tensor(out=fused[c % 2][:, m], in0=u_ps[n % 2][:],
                                                 scalar=s_up[:, 1, m:m + 1], in1=gate[n % 2][:],
                                                 op0=ALU.mult, op1=ALU.mult).then_inc(fuse, 1)
                if c >= 1:
                    close(c - 1)


H1, D1 = 4, 64
ROT = D1 // 2


def retention_tables():
    import numpy as np
    inv = 1.0 / 10000.0 ** (np.arange(0, ROT, 2, dtype=np.float64) / ROT)
    t = np.arange(SEQ, dtype=np.float64)
    freqs = np.repeat(t[:, None] * inv[None, :], 2, axis=-1)
    base = (np.arange(0, ROT, 2, dtype=np.float64) + 0.4 * ROT) / (1.4 * ROT)
    scale = base[None, :] ** ((t - SEQ // 2) / 512.0)[:, None]
    scale = np.concatenate([scale, scale], axis=-1)
    sign = np.where(np.arange(ROT) % 2 == 0, -1.0, 1.0)
    out = np.zeros((2, 2, E, SEQ))
    for h in range(H1):
        decay = (1.0 - 2.0 ** (-5.0 - h)) ** t
        for side, (sc, dc) in enumerate(((scale, decay), (1.0 / scale, 1.0 / decay))):
            r = h * D1
            out[side, 0, r:r + ROT] = (np.cos(freqs) * sc).T * dc
            out[side, 1, r:r + ROT] = (np.sin(freqs) * sc * sign).T * dc
            out[side, 0, r + ROT:r + D1] = dc
    return out.astype(np.float32)


def retention(nc, a, keep):
    with ExitStack() as ctx:
        sb, ps, sem = scope(nc, ctx, "ret")
        x_t = keep["x_t"]
        w = sb("w", [P, 5, KT, E])
        tab = [sb(f"tab{i}", [P, 2, 2, CH]) for i in range(2)]
        qk_t = sb("qk_t", [P, 2, KT, TOK])
        mish = sb("mish", [P, KT, TOK])
        v = sb("v", [P, NT, E])
        k_tok = sb("k_tok", [P, NT, E])
        ret = sb("ret", [P, KT, TOK])
        raw, swapped, part = (sb(n, [P, 2, CH]) for n in ("raw", "swapped", "part"))
        g_min, g_exp, g_num = (sb(n, [P, 2, CH]) for n in ("g_min", "g_exp", "g_num"))
        causal = sb("causal", [P, 2, P])
        masked = [sb(f"masked{i}", [P, 2, 2, P]) for i in range(2)]
        state = [sb(f"state{i}", [P, KT, P]) for i in range(2)]
        blocks1 = sb("blocks1", [P, P])
        gn = sb("gn", [P, 2, KT])
        gstat = sb("gstat", [P, KT * BATCH, 2, 6])
        gmv = sb("gmv", [P, KT * BATCH, 2])
        gtmp = sb("gtmp", [P, 6, KT * BATCH])
        banks = [ps(f"b{i}") for i in range(6)]
        norm = norm_parts((sb, ps, sem), keep)
        g_ps = norm["turn_ps"]

        weights, tables = sem("weights"), [sem(f"tables{i}") for i in range(2)]
        consts = sem("consts")
        projected, raw_in, swap_done, sin_done, cos_done, rot_done = (sem(n) for n in (
            "projected", "raw_in", "swap_done", "sin_done", "cos_done", "rot_done"))
        g_made, g_raw, g_low, g_e, g_n, g_d, g_r, g_q, g_done = (sem(n) for n in (
            "g_made", "g_raw", "g_low", "g_e", "g_n", "g_d", "g_r", "g_q", "g_done"))
        v_made, v_in, k_turned, k_in = (sem(n) for n in ("v_made", "v_in", "k_turned", "k_in"))
        scored, mask_done, state_made, state_in, ret_made, ret_in = (sem(n) for n in (
            "scored", "mask_done", "state_made", "state_in", "ret_made", "ret_in"))
        gchain, gsq, ggroup, groot, gpow = (sem(n) for n in ("gchain", "gsq", "ggroup", "groot", "gpow"))
        applied, weighed, made = (sem(n) for n in ("applied", "weighed", "made"))

        rot = [(c, side, m) for c in range(NCH) for m in range(KT) for side in range(2)]
        gates = [(c, m) for c in range(NCH) for m in range(KT)]
        assert 2 * len(gates) == NT
        block = ctx.enter_context(nc.Block())

        @block.sync
        def _(sp):
            for i, name in enumerate(("w_q1", "w_k1", "w_g1", "w_v1", "w_o1")):
                sp.dma_start(w[:, i], a[name].rearrange("(k p) n -> p k n", p=P)).then_inc(weights, 16)
            for n in range(NCH * KT):
                c, m = n // KT, n % KT
                if n >= 2:
                    sp.wait_ge(cos_done, 2 * (n - 1))
                    sp.wait_ge(sin_done, 2 * (n - 1))
                cc = c % QC
                for side in range(2):
                    sp.dma_start(tab[n % 2][:, side],
                                 a["tables"][side, :, m * P:(m + 1) * P, cc * CH:(cc + 1) * CH]
                                 .rearrange("f p t -> p f t")).then_inc(tables[n % 2], 16)
            sp.dma_start(gn[:, 0], a["gn_w"]).then_inc(consts, 16)
            sp.dma_start(gn[:, 1], a["gn_b"]).then_inc(consts, 16)

        @block.gpsimd
        def _(pool):
            pool.memset(causal[:], 1.0).then_inc(groot, 1)
            pool.memset(blocks1[:], 0.0).then_inc(groot, 1)
            pool.wait_ge(groot, 2)
            pool.affine_select(out=causal[:], in_=causal[:], compare_op=ALU.is_ge, fill=0.0,
                               base=0, pattern=[[0, 2], [1, P]], channel_multiplier=-1).then_inc(groot, 1)
            for i in range(2):
                pool.wait_ge(groot, 3 + i)
                pool.memset(blocks1[i * D1:(i + 1) * D1, i * D1:(i + 1) * D1], 1.0 / D1).then_inc(groot, 1)
            for i in range(2):
                pool.wait_ge(groot, 5 + i)
                pool.memset(state[i][:], 0.0).then_inc(groot, 1)
            pool.wait_ge(groot, 7)
            for n, (c, side, m) in enumerate(rot):
                pool.wait_ge(cos_done, n + 1)
                pool.wait_ge(sin_done, n + 1)
                pool.tensor_tensor(qk_t[:, side, m, c * CH:(c + 1) * CH], part[:, n % 2], swapped[:, n % 2],
                                   ALU.add).then_inc(rot_done, 1)
            for n, (c, m) in enumerate(gates):
                pool.wait_ge(g_r, n + 1)
                pool.tensor_tensor(g_num[:, n % 2], g_num[:, n % 2], g_exp[:, n % 2], ALU.mult).then_inc(g_q, 1)
            pool.wait_ge(gsq, 6)
            pool.tensor_tensor(gtmp[:, 3], gtmp[:, 2], norm["half"][:, 0:KT * BATCH], ALU.pow).then_inc(gpow, 1)
            for c in range(NCH):
                norm_root(pool, norm, c)

        @block.tensor
        def _(pe):
            pe.wait_ge(weights, 80)
            for n, (c, side, m) in enumerate(rot):
                if n >= 2:
                    pe.wait_ge(cos_done, n - 1)
                    pe.wait_ge(raw_in, n - 1)
                for k in range(KT):
                    mm = pe.matmul(banks[n % 2][:], w[:, side, k, m * P:(m + 1) * P],
                                   x_t[:, k, c * CH:(c + 1) * CH], start=(k == 0), stop=(k == KT - 1))
                mm.then_inc(projected, 1)
            for t in range(NT):
                if t >= 2:
                    pe.wait_ge(v_in, t - 1)
                for k in range(KT):
                    mm = pe.matmul(banks[4 + t % 2][:, 0:E], x_t[:, k, t * P:(t + 1) * P], w[:, 3, k],
                                   start=(k == 0), stop=(k == KT - 1))
                mm.then_inc(v_made, 1)
            pe.wait_ge(rot_done, len(rot))
            for t in range(NT):
                if t >= 2:
                    pe.wait_ge(k_in, t - 1)
                for m in range(KT):
                    mm = pe.transpose(banks[t % 2][:, m * P:(m + 1) * P], qk_t[:, 1, m, t * P:(t + 1) * P],
                                      keep["ident"][:])
                mm.then_inc(k_turned, 1)
            pe.wait_ge(v_in, NT)
            pe.wait_ge(k_in, NT)

            def scores(t):
                if t >= 1:
                    pe.wait_ge(mask_done, 2 * t)
                for h in range(H1):
                    r, m = D1 * (h % 2), h // 2
                    mm = pe.matmul(banks[h % 2][:, m * P:(m + 1) * P], qk_t[r:r + D1, 1, m, t * P:(t + 1) * P],
                                   qk_t[r:r + D1, 0, m, t * P:(t + 1) * P], start=True, stop=True)
                mm.then_inc(scored, 1)

            def gate(n):
                c, m = gates[n]
                if n >= 2:
                    pe.wait_ge(g_low, n - 1)
                for k in range(KT):
                    mm = pe.matmul(g_ps[n % 2][:], w[:, 2, k, m * P:(m + 1) * P],
                                   x_t[:, k, c * CH:(c + 1) * CH], start=(k == 0), stop=(k == KT - 1))
                mm.then_inc(g_made, 1)

            scores(0)
            for t in range(NT):
                n = t % KTS
                if t:
                    pe.wait_ge(state_in, t)
                for h in range(H1):
                    r, m = D1 * (h % 2), h // 2
                    mm = pe.matmul(banks[4 + m][r:r + D1, 0:D1], k_tok[:, t, h * D1:(h + 1) * D1],
                                   v[:, t, h * D1:(h + 1) * D1], start=(n == 0), stop=(n == KTS - 1),
                                   skip_group_check=True)
                mm.then_inc(state_made, 1)
                if t + 1 < NT:
                    scores(t + 1)
                if t % 2 == 0:
                    gate(t // 2)
                pe.wait_ge(mask_done, 2 * t + 2)
                if t >= 2:
                    pe.wait_ge(ret_in, t - 1)
                if n:
                    pe.wait_ge(state_in, t)
                for m in range(KT):
                    out = banks[2 + t % 2][:, m * P:(m + 1) * P]
                    for i in range(2):
                        r, h = D1 * i, 2 * m + i
                        mm = pe.matmul(out[r:r + D1], v[:, t, h * D1:(h + 1) * D1], masked[t % 2][:, i, m],
                                       start=True, stop=(n == 0))
                    if n:
                        mm = pe.matmul(out, state[(t - 1) % 2][:, m], qk_t[:, 0, m, t * P:(t + 1) * P],
                                       start=False, stop=True)
                mm.then_inc(ret_made, 1)
            pe.wait_ge(gsq, 2)
            pe.matmul(banks[0][:, 0:2 * KT * BATCH], blocks1[:], gmv[:].rearrange("p a b -> p (a b)"),
                      start=True, stop=True).then_inc(ggroup, 1)
            for c in range(NCH + LAG):
                if c < NCH:
                    for t in range(c * TC, (c + 1) * TC):
                        b = t // KTS
                        pe.wait_ge(weighed, KT * (b + 1))
                        if t >= 2:
                            pe.wait_ge(norm["summed"], t - 1)
                        for k in range(KT):
                            mm = pe.matmul(banks[4 + t % 2][:, 0:E], ret[:, k, t * P:(t + 1) * P], w[:, 4, k],
                                           start=(k == 0), stop=(k == KT - 1))
                        mm.then_inc(made, 1)
                if c >= LAG:
                    norm_turn(pe, norm, c - LAG)

        @block.scalar
        def _(act):
            for n, (c, side, m) in enumerate(rot):
                act.wait_ge(projected, n + 1)
                if n >= 2:
                    act.wait_ge(swap_done, n - 1)
                act.activation(raw[:, n % 2], banks[n % 2][:], ACT.Copy).then_inc(raw_in, 1)
            for t in range(NT):
                act.wait_ge(v_made, t + 1)
                act.activation(v[:, t], banks[4 + t % 2][:, 0:E], ACT.Copy).then_inc(v_in, 1)
            for t in range(NT):
                act.wait_ge(k_turned, t + 1)
                act.activation(k_tok[:, t], banks[t % 2][:, 0:E], ACT.Copy).then_inc(k_in, 1)
            for t in range(NT):
                if t % 2 == 0:
                    n = t // 2
                    c, m = gates[n]
                    act.wait_ge(g_made, n + 1)
                    act.activation(mish[:, m, c * CH:(c + 1) * CH], g_ps[n % 2][:], ACT.Copy).then_inc(g_raw, 1)
                    act.wait_ge(g_low, n + 1)
                    if n >= 2:
                        act.wait_ge(g_q, n - 1)
                    act.activation(g_exp[:, n % 2], g_min[:, n % 2], ACT.Exp).then_inc(g_e, 1)
                act.wait_ge(ret_made, t + 1)
                act.activation(ret[:, :, t * P:(t + 1) * P], banks[2 + t % 2][:, 0:KT * P].rearrange(
                    "p (m t) -> p m t", m=KT), ACT.Copy).then_inc(ret_in, 1)
            for c in range(NCH):
                norm_keep(act, norm, c)

        @block.vector
        def _(dve):
            swap = [i ^ 1 for i in range(32)]
            for n, (c, side, m) in enumerate(rot):
                dve.wait_ge(raw_in, n + 1)
                if n >= 2:
                    dve.wait_ge(rot_done, n - 1)
                dve.stream_shuffle(swapped[:, n % 2], raw[:, n % 2], swap).then_inc(swap_done, 1)
                dve.wait_ge(tables[(n // 2) % 2], 32 * (n // 4 + 1))
                dve.tensor_tensor(part[:, n % 2], banks[n % 2][:], tab[(n // 2) % 2][:, side, 0],
                                  ALU.mult).then_inc(cos_done, 1)
                dve.wait_ge(swap_done, n + 1)
                dve.tensor_tensor(swapped[:, n % 2], swapped[:, n % 2], tab[(n // 2) % 2][:, side, 1],
                                  ALU.mult).then_inc(sin_done, 1)
            def gate_parts(n):
                dve.wait_ge(g_raw, n + 1)
                if n >= 2:
                    dve.wait_ge(g_e, n - 1)
                dve.tensor_scalar(g_min[:, n % 2], g_ps[n % 2][:], 20.0, None, ALU.min).then_inc(g_low, 1)
                dve.wait_ge(g_e, n + 1)
                if n >= 2:
                    dve.wait_ge(g_done, n - 1)
                dve.scalar_tensor_tensor(out=g_num[:, n % 2], in0=g_exp[:, n % 2], scalar=2.0, in1=g_exp[:, n % 2],
                                         op0=ALU.add, op1=ALU.mult).then_inc(g_n, 1)
                dve.wait_ge(g_n, n + 1)
                dve.tensor_scalar(g_exp[:, n % 2], g_num[:, n % 2], 2.0, None, ALU.add).then_inc(g_d, 1)

            def gate_inverse(n):
                dve.wait_ge(g_d, n + 1)
                dve.reciprocal(g_exp[:, n % 2], g_exp[:, n % 2]).then_inc(g_r, 1)

            def gate_close(n):
                c, m = gates[n]
                dve.wait_ge(g_q, n + 1)
                dve.tensor_tensor(mish[:, m, c * CH:(c + 1) * CH], mish[:, m, c * CH:(c + 1) * CH],
                                  g_num[:, n % 2], ALU.mult).then_inc(g_done, 1)

            dve.wait_ge(groot, 7)
            for t in range(NT):
                dve.wait_ge(scored, t + 1)
                if t >= 2:
                    dve.wait_ge(ret_made, t - 1)
                for i in range(2):
                    dve.tensor_tensor(masked[t % 2][:, i], banks[i][:, 0:KT * P].rearrange("p (m t) -> p m t", m=KT),
                                      causal[:], ALU.mult).then_inc(mask_done, 1)
                dve.wait_ge(state_made, t + 1)
                if t >= 2:
                    dve.wait_ge(ret_made, t)
                for m in range(KT):
                    for r in (0, D1):
                        cp = dve.tensor_copy(state[t % 2][r:r + D1, m, r:r + D1], banks[4 + m][r:r + D1, 0:D1])
                cp.then_inc(state_in, 1)
                if t % 2 == 0:
                    if t >= 2:
                        gate_close(t // 2 - 1)
                    gate_parts(t // 2)
                else:
                    gate_inverse(t // 2)
            gate_close(len(gates) - 1)
            for b in range(BATCH):
                for m in range(KT):
                    i = b * KT + m
                    dve.wait_ge(ret_in, KTS * (b + 1))
                    for c in range(QC):
                        st = dve.bn_stats(gstat[:, i, c], ret[:, m, b * SEQ + c * CH:b * SEQ + (c + 1) * CH])
                    st.then_inc(gchain, 1)
            for i in range(KT * BATCH):
                dve.wait_ge(gchain, i + 1)
                ag = dve.bn_aggr(gmv[:, i], gstat[:, i].rearrange("p a b -> p (a b)"))
            ag.then_inc(gchain, 1)
            dve.wait_ge(gchain, KT * BATCH + 1)
            mean, var = gmv[:, :, 0], gmv[:, :, 1]
            dve.tensor_tensor(gtmp[:, 0], mean, mean, ALU.mult).then_inc(gsq, 1)
            dve.wait_ge(gsq, 1)
            dve.tensor_tensor(var, var, gtmp[:, 0], ALU.add).then_inc(gsq, 1)
            dve.wait_ge(ggroup, 1)
            group = banks[0][:, 0:2 * KT * BATCH].rearrange("p (a b) -> p a b", b=2)
            dve.tensor_copy(gtmp[:, 1], group[:, :, 0]).then_inc(gsq, 1)
            dve.wait_ge(gsq, 3)
            dve.tensor_tensor(gtmp[:, 0], gtmp[:, 1], gtmp[:, 1], ALU.mult).then_inc(gsq, 1)
            dve.wait_ge(gsq, 4)
            dve.tensor_tensor(gtmp[:, 2], group[:, :, 1], gtmp[:, 0], ALU.subtract).then_inc(gsq, 1)
            dve.wait_ge(gsq, 5)
            dve.tensor_scalar(gtmp[:, 2], gtmp[:, 2], 0.0, EPS, ALU.max, ALU.add).then_inc(gsq, 1)
            dve.wait_ge(gpow, 1)
            dve.wait_ge(consts, 32)
            for b in range(BATCH):
                dve.tensor_tensor(gtmp[:, 4, b * KT:(b + 1) * KT], gtmp[:, 3, b * KT:(b + 1) * KT], gn[:, 0],
                                  ALU.mult).then_inc(gsq, 1)
            dve.wait_ge(gsq, 8)
            dve.tensor_tensor(gtmp[:, 0], gtmp[:, 1], gtmp[:, 4], ALU.mult).then_inc(gsq, 1)
            dve.wait_ge(gsq, 9)
            for b in range(BATCH):
                dve.tensor_tensor(gtmp[:, 5, b * KT:(b + 1) * KT], gn[:, 1], gtmp[:, 0, b * KT:(b + 1) * KT],
                                  ALU.subtract).then_inc(gsq, 1)
            dve.wait_ge(gsq, 11)
            dve.wait_ge(g_done, len(gates))
            for b in range(BATCH):
                for m in range(KT):
                    i = b * KT + m
                    r = ret[:, m, b * SEQ:(b + 1) * SEQ]
                    dve.tensor_scalar(r, r, gtmp[:, 4, i:i + 1], gtmp[:, 5, i:i + 1], ALU.mult,
                                      ALU.add).then_inc(applied, 1)
                    dve.wait_ge(applied, i + 1)
                    dve.tensor_tensor(r, r, mish[:, m, b * SEQ:(b + 1) * SEQ], ALU.mult).then_inc(weighed, 1)
            for c in range(NCH):
                for t in range(c * TC, (c + 1) * TC):
                    dve.wait_ge(made, t + 1)
                    norm_add(dve, norm, t, banks[4 + t % 2][:, 0:E])
                norm_measure(dve, norm, c)
                norm_scale(dve, norm, c)


EXPERTS, TOP, WIDE = 64, 6, 176
HALF = WIDE // 2
HPAD = 96
SHARED = 2 * WIDE
SH_TILES = (128, 128, 96)
TILES = -(-(TOK * TOP // P + EXPERTS) // 8) * 8
assert sum(SH_TILES) == SHARED


def route(nc, a, keep):
    with ExitStack() as ctx:
        sb, ps, sem = scope(nc, ctx, "route")
        x, x_t = keep["x"], keep["x_t"]
        weight, slot_i, tok_i, owner = (keep[n] for n in ("weight", "slot_i", "tok_i", "owner"))
        w_r = sb("w_r", [P, KT, EXPERTS])
        logit = sb("logit", [P, NT, EXPERTS])
        best = sb("best", [P, NT, 8])
        best_i = sb("best_i", [P, NT, 8], U32)
        best_f = sb("best_f", [P, NT, 8], BF16)
        expo = sb("expo", [P, NT, TOP])
        esum = sb("esum", [P, NT])
        iota = sb("iota", [P, TILES], BF16)
        lane = sb("lane", [P, 1])
        tile_no = sb("tile_no", [P, 2])
        chosen = sb("chosen", [P, TOP, NT, EXPERTS], BF16)
        member = sb("member", [P, NT, EXPERTS], BF16)
        sums = sb("sums", [P, NT + 1, EXPERTS], BF16)
        before = sb("before", [P, P], BF16)
        upto = sb("upto", [P, P], BF16)
        ones = sb("ones", [P, P], BF16)
        count_i = sb("count_i", [EXPERTS, 2], I32)
        n_tiles = sb("n_tiles", [EXPERTS, P], BF16)
        base = sb("base", [P, EXPERTS])
        ends = sb("ends", [P, EXPERTS])
        place = sb("place", [P, NT, EXPERTS])
        pick = sb("pick", [P, NT, EXPERTS])
        slot = sb("slot", [P, NT, TOP])
        low_i, high_i = sb("low_i", [P, NT, TOP], I32), sb("high_i", [P, NT, TOP], I32)
        low, high = sb("low", [P, NT, TOP]), sb("high", [P, NT, TOP])
        HOTS = 16
        hot_low = sb("hot_low", [P, HOTS, P], BF16)
        hot_high = sb("hot_high", [P, HOTS, 2, TILES], BF16)
        tok_f = sb("tok_f", [P, TILES])
        past = sb("past", [P, 2, EXPERTS])
        owner_f, owner_i = sb("owner_f", [P, 2]), sb("owner_i", [P, 2], I32)
        l_ps = [ps(f"l{i}") for i in range(2)]
        m_ps = ps("m")
        w_r_in, x_out = sem("w_r_in"), sem("x_out")
        consts, lg_made, lg_in, best_in, bi_in, vc = (sem(n) for n in (
            "consts", "lg_made", "lg_in", "best_in", "bi_in", "vc"))
        exp_in, placed, counted, based, owned, owner_out, owner_in = (sem(n) for n in (
            "exp_in", "placed", "counted", "based", "owned", "owner_out", "owner_in"))
        split, hot_low_in, hot_in, hot_used = (sem(n) for n in ("split", "hot_low_in", "hot_in", "hot_used"))
        PER_BANK = CH // EXPERTS
        pairs = [(t, k) for t in range(NT) for k in range(TOP)]
        A_VC = 8 + TOP - 1 + NT
        block = ctx.enter_context(nc.Block())

        @block.sync
        def _(sp):
            sp.dma_start(w_r[:], a["w_router"].rearrange("(k p) n -> p k n", p=P)).then_inc(w_r_in, 16)
            sp.dma_start(a["x_rows"].rearrange("(t p) n -> p t n", p=P), x[:]).then_inc(x_out, 16)
            sp.wait_ge(owned, 1)
            sp.dma_start(a["owners"].rearrange("(p a) -> p a", p=P), owner_i[:]).then_inc(owner_out, 16)
            sp.wait_ge(owner_out, 16)
            sp.dma_start(owner[:], a["owners"].rearrange("(o n) -> o n", o=1)).then_inc(owner_in, 16)
            sp.wait_ge(owner_in, 16)
            sp.wait_ge(x_out, 16)

        @block.gpsimd
        def _(pool):
            done = 0

            def ordered(instruction):
                nonlocal done
                instruction.then_inc(consts, 1)
                done += 1
                pool.wait_ge(consts, done)

            ordered(pool.iota(iota[:], pattern=[[1, TILES]], base=0, channel_multiplier=0,
                              allow_small_or_imprecise_dtypes=True))
            ordered(pool.iota(lane[:], pattern=[[1, 1]], base=0, channel_multiplier=1,
                              allow_small_or_imprecise_dtypes=True))
            ordered(pool.iota(tile_no[:], pattern=[[1, 2]], base=0, channel_multiplier=2,
                              allow_small_or_imprecise_dtypes=True))
            ordered(pool.memset(ones[:], 1.0))
            ordered(pool.memset(before[:], 1.0))
            ordered(pool.memset(upto[:], 1.0))
            ordered(pool.affine_select(out=before[:], in_=before[:], compare_op=ALU.is_gt, fill=0.0,
                                       base=0, pattern=[[1, P]], channel_multiplier=-1))
            ordered(pool.affine_select(out=upto[:], in_=upto[:], compare_op=ALU.is_ge, fill=0.0,
                                       base=0, pattern=[[1, P]], channel_multiplier=-1))
            ordered(pool.memset(sums[:, 0], 0.0))
            pool.wait_ge(split, 1)
            for n, (t, k) in list(enumerate(pairs))[1::2]:
                if n >= HOTS:
                    pool.wait_ge(hot_used, n - HOTS + 1)
                pool.tensor_scalar(hot_low[:, n % HOTS], iota[:, 0:P], low[:, t, k:k + 1], None,
                                   ALU.is_equal).then_inc(hot_low_in, 1)

        @block.tensor
        def _(pe):
            pe.wait_ge(w_r_in, 16)
            for t in range(NT):
                for k in range(KT):
                    mm = pe.matmul(l_ps[t // PER_BANK][:, t % PER_BANK * EXPERTS:(t % PER_BANK + 1) * EXPERTS],
                                   x_t[:, k, t * P:(t + 1) * P], w_r[:, k], start=(k == 0), stop=(k == KT - 1))
                mm.then_inc(lg_made, 1)

            pe.wait_ge(consts, 9)
            pe.wait_ge(vc, A_VC)
            pe.wait_ge(lg_in, 2)
            for t in range(NT):
                out = l_ps[t // PER_BANK][:, t % PER_BANK * EXPERTS:(t % PER_BANK + 1) * EXPERTS]
                pe.matmul(out, before[:], member[:, t], start=True, stop=False)
                mm = pe.matmul(out, ones[:], sums[:, t], start=False, stop=True)
            mm.then_inc(placed, 1)
            pe.matmul(m_ps[0:EXPERTS, 0:1], sums[:, NT], ones[:, 0:1], start=True, stop=True).then_inc(counted, 1)
            pe.wait_ge(vc, A_VC + 3)
            pe.matmul(m_ps[:, 0:EXPERTS], n_tiles[:], before[0:EXPERTS, 0:EXPERTS], start=True, stop=True)
            pe.matmul(m_ps[:, EXPERTS:2 * EXPERTS], n_tiles[:], upto[0:EXPERTS, 0:EXPERTS],
                      start=True, stop=True).then_inc(based, 1)
            pe.wait_ge(vc, A_VC + 5)
            for n, (t, k) in enumerate(pairs):
                pe.wait_ge(hot_in, n + 1)
                if n % 2:
                    pe.wait_ge(hot_low_in, n // 2 + 1)
                pe.matmul(m_ps[:, 0:2 * TILES], hot_low[:, n % HOTS],
                          hot_high[:, n % HOTS].rearrange("p a j -> p (a j)"),
                          start=(n == 0), stop=(n == len(pairs) - 1)).then_inc(hot_used, 1)

        @block.scalar
        def _(act):
            for i in range(2):
                act.wait_ge(lg_made, PER_BANK * (i + 1))
                act.activation(logit[:, i * PER_BANK:(i + 1) * PER_BANK], l_ps[i][:].rearrange(
                    "p (t e) -> p t e", e=EXPERTS), ACT.Copy).then_inc(lg_in, 1)

            act.wait_ge(vc, 3)
            act.activation(expo[:], expo[:], ACT.Exp).then_inc(exp_in, 1)

        @block.vector
        def _(dve):
            steps = 0

            def chain(instruction):
                nonlocal steps
                instruction.then_inc(vc, 1)
                steps += 1
                dve.wait_ge(vc, steps)

            for t in range(NT):
                dve.wait_ge(lg_in, t // PER_BANK + 1)
                dve.max(best[:, t], logit[:, t]).then_inc(best_in, 1)
            for t in range(NT):
                dve.wait_ge(best_in, t + 1)
                dve.max_index(best_i[:, t], best[:, t], logit[:, t]).then_inc(bi_in, 1)
            dve.wait_ge(bi_in, NT)
            chain(dve.tensor_copy(best_f[:], best_i[:]))
            dve.wait_ge(consts, 9)
            chain(dve.memset(esum[:], 0.0))
            chain(dve.tensor_tensor(expo[:], best[:, :, 0:TOP], best[:, :, 0:1].to_broadcast([P, NT, TOP]),
                                    ALU.subtract))
            dve.wait_ge(exp_in, 1)
            chain(dve.tensor_reduce(esum[:], expo[:], AX.X, ALU.add))
            chain(dve.reciprocal(esum[:], esum[:]))
            chain(dve.tensor_tensor(weight[:], expo[:], esum[:].unsqueeze(2).to_broadcast([P, NT, TOP]), ALU.mult))
            for k in range(TOP):
                op = dve.tensor_tensor(chosen[:, k], iota[:, 0:EXPERTS].unsqueeze(1).to_broadcast([P, NT, EXPERTS]),
                                       best_f[:, :, k:k + 1].to_broadcast([P, NT, EXPERTS]), ALU.is_equal)
            chain(op)
            chain(dve.tensor_copy(member[:], chosen[:, 0]))
            for k in range(1, TOP):
                chain(dve.tensor_tensor(member[:], member[:], chosen[:, k], ALU.add))
            for t in range(NT):
                chain(dve.tensor_tensor(sums[:, t + 1], sums[:, t], member[:, t], ALU.add))
            assert steps == A_VC
            dve.wait_ge(counted, 1)
            chain(dve.tensor_scalar(count_i[:, 0:1], m_ps[0:EXPERTS, 0:1], float(P - 1), None, ALU.add))
            chain(dve.tensor_single_scalar(count_i[:, 1:2], count_i[:, 0:1], 7, ALU.logical_shift_right))
            chain(dve.tensor_copy(n_tiles[:], count_i[:, 1:2].to_broadcast([EXPERTS, P])))
            dve.wait_ge(based, 1)
            chain(dve.tensor_scalar(base[:], m_ps[:, 0:EXPERTS], float(P), None, ALU.mult))
            chain(dve.tensor_copy(ends[:], m_ps[:, EXPERTS:2 * EXPERTS]))
            for i in range(2):
                chain(dve.tensor_scalar(past[:, i], ends[:], tile_no[:, i:i + 1], None, ALU.is_le))
            chain(dve.tensor_reduce(owner_f[:], past[:], AX.X, ALU.add))
            chain(dve.tensor_scalar(owner_f[:], owner_f[:], float(EXPERTS - 1), None, ALU.min))
            dve.tensor_copy(owner_i[:], owner_f[:]).then_inc(owned, 1)
            dve.wait_ge(placed, 1)
            for i in range(2):
                chain(dve.tensor_tensor(place[:, i * PER_BANK:(i + 1) * PER_BANK],
                                        l_ps[i][:].rearrange("p (t e) -> p t e", e=EXPERTS),
                                        base[:].unsqueeze(1).to_broadcast([P, PER_BANK, EXPERTS]), ALU.add))
            for k in range(TOP):
                chain(dve.tensor_tensor(pick[:], place[:], chosen[:, k], ALU.mult))
                chain(dve.tensor_reduce(slot[:, :, k], pick[:], AX.X, ALU.add))
            chain(dve.tensor_copy(slot_i[:], slot[:]))
            chain(dve.tensor_single_scalar(low_i[:], slot_i[:], P - 1, ALU.bitwise_and))
            chain(dve.tensor_single_scalar(high_i[:], slot_i[:], 7, ALU.logical_shift_right))
            chain(dve.tensor_copy(low[:], low_i[:]))
            dve.tensor_copy(high[:], high_i[:]).then_inc(split, 1)
            dve.wait_ge(split, 1)
            for n, (t, k) in enumerate(pairs):
                if n >= HOTS:
                    dve.wait_ge(hot_used, n - HOTS + 1)
                if n % 2 == 0:
                    dve.tensor_scalar(hot_low[:, n % HOTS], iota[:, 0:P], low[:, t, k:k + 1], None, ALU.is_equal)
                dve.tensor_scalar(hot_high[:, n % HOTS, 0], iota[:], high[:, t, k:k + 1], float(t),
                                  ALU.is_equal, ALU.mult)
                dve.tensor_scalar(hot_high[:, n % HOTS, 1], iota[:], high[:, t, k:k + 1], lane[:, 0:1],
                                  ALU.is_equal, ALU.mult).then_inc(hot_in, 1)
            dve.wait_ge(hot_used, len(pairs))
            chain(dve.tensor_scalar(tok_f[:], m_ps[:, 0:TILES], float(P), None, ALU.mult))
            chain(dve.tensor_tensor(tok_f[:], m_ps[:, TILES:2 * TILES], tok_f[:], ALU.add))
            chain(dve.tensor_copy(tok_i[:], tok_f[:]))

def experts(nc, a, keep):
    with ExitStack() as ctx:
        sb, ps, sem = scope(nc, ctx, "exp")
        tok_i, owner, ident = keep["tok_i"], keep["owner"], keep["ident"]
        UN = 32
        B = 4
        TURNS = TILES // UN
        w1 = [sb(f"w1_{i}", [P, KT, 2, HALF]) for i in range(B)]
        w2 = [sb(f"w2_{i}", [HPAD, 2, E]) for i in range(B)]
        idx = [sb(f"idx{i}", [P, B], I32) for i in range(UN // B)]
        spare = sb("spare", [P, 1])
        rows = [sb(f"rows{i}", [P, E]) for i in range(B)]
        xt = [sb(f"xt{i}", [P, KT, P]) for i in range(2)]
        ht = [sb(f"ht{i}", [HPAD, 2, P]) for i in range(2)]
        y_sb = [sb(f"y_sb{i}", [P, E]) for i in range(B)]
        xt_ps = [ps(f"xt_ps{i}") for i in range(2)]
        h_ps = [ps(f"h_ps{i}") for i in range(2)]
        y_ps = [ps(f"y_ps{i}") for i in range(2)]
        w_in = [sem(f"w_in{i}") for i in range(B)]
        turned = [sem(f"turned{i}") for i in range(B)]
        y_made = [sem(f"y_made{i}") for i in range(B)]
        rows_in = [sem(f"rows_in{i}") for i in range(B)]
        y_out = [sem(f"y_out{i}") for i in range(B)]
        padded, idx_in, stepped = sem("padded"), sem("idx_in"), sem("stepped")
        xt_in, h_made, h_in, y_in = (sem(n) for n in ("xt_in", "h_made", "h_in", "y_in"))
        block = ctx.enter_context(nc.Block())

        def nth(i, b):
            return i * (UN // B) + b // B

        @block.sync
        def _(sp):
            sp.wait_ge(padded, 2 + B)
            with sp.Fori(0, TURNS) as i:
                for b in range(UN):
                    n = b % B
                    e = sp.value_load(owner[0:1, bass.ds(i * UN + b, 1)], min_val=0, max_val=EXPERTS - 1)
                    sp.wait_ge(y_made[n], CREDIT + nth(i, b))
                    sp.dma_start(w1[n][:], a["w1"][e].rearrange("p (k j n) -> p k j n", k=KT, j=2)
                                 ).then_inc(w_in[n], 16)
                    sp.dma_start(w2[n][0:HALF], a["w2"][e].rearrange("p (j n) -> p j n", j=2)).then_inc(w_in[n], 16)
            for n in range(B):
                sp.wait_ge(w_in[n], 32 * (TILES // B))

        @block.gpsimd
        def _(pool):
            pool.sem_inc(stepped, CREDIT)
            with pool.Fori(0, TURNS) as i:
                steps = 0

                def held(semaphore, value):
                    nonlocal steps
                    pool.wait_ge(semaphore, value)
                    pool.wait_ge(stepped, CREDIT + i * (UN // B * (B + 1)) + steps)
                    pool.tensor_tensor(spare[:], ident[:, 0:1], ident[:, 1:2], ALU.add).then_inc(stepped, 1)
                    steps += 1

                for b in range(UN):
                    n, half = b % B, b // B
                    held(turned[n], CREDIT + nth(i, b))
                    if n == 0:
                        pool.tensor_copy(idx[half][:], tok_i[:, bass.ds(i * UN + b, B)]).then_inc(idx_in, 1)
                        held(idx_in, i * (UN // B) + (half + 1))
                    pool.indirect_dma_start(rows[n][:], None, a["x_rows"], bass.IndirectOffsetOnAxis(
                        ap=idx[half][:, n:n + 1], axis=0)).then_inc(rows_in[n], 16)
            pool.wait_ge(turned[0], CREDIT + TILES // B)
            pool.wait_ge(stepped, CREDIT + TILES // B * (B + 1))
            pool.tensor_tensor(spare[:], ident[:, 0:1], ident[:, 1:2], ALU.add).then_inc(stepped, 1)
            pool.indirect_dma_start(rows[0][:], None, a["x_rows"], bass.IndirectOffsetOnAxis(
                ap=idx[0][:, 0:1], axis=0)).then_inc(rows_in[0], 16)
            for n in range(B):
                pool.wait_ge(rows_in[n], 16 * (TILES // B + (n == 0)))

        @block.tensor
        def _(pe):
            for semaphore in turned + y_made + [h_made]:
                pe.sem_inc(semaphore, CREDIT)
            pe.wait_ge(padded, B + 2)
            def turn(i, b):
                n = b % B
                pe.wait_ge(rows_in[n], 16 * nth(i, b) + 16)
                pe.wait_ge(xt_in, CREDIT + i * UN + max(0, b - 1))
                for k in range(KT):
                    mm = pe.transpose(xt_ps[b % 2][:, k * P:(k + 1) * P], rows[n][:, k * P:(k + 1) * P], ident[:])
                mm.then_inc(turned[n], 1)

            turn(0, 0)
            with pe.Fori(0, TURNS) as i:
                def up(b):
                    n = b % B
                    pe.wait_ge(w_in[n], 32 * nth(i, b) + 32)
                    pe.wait_ge(xt_in, CREDIT + i * UN + (b + 1))
                    pe.wait_ge(h_in, CREDIT + i * UN + max(0, b - 1))
                    for j in range(2):
                        for k in range(KT):
                            mm = pe.matmul(h_ps[b % 2][0:HALF, j * P:(j + 1) * P], w1[n][:, k, j], xt[b % 2][:, k],
                                           start=(k == 0), stop=(k == KT - 1))
                    mm.then_inc(h_made, 1)

                def down(b):
                    n = b % B
                    pe.wait_ge(h_in, CREDIT + i * UN + (b + 1))
                    pe.wait_ge(y_in, CREDIT + i * UN + max(0, b - 1))
                    for j in range(2):
                        mm = pe.matmul(y_ps[b % 2][:, 0:E], ht[b % 2][:, j], w2[n][:, j], start=(j == 0), stop=(j == 1))
                    mm.then_inc(y_made[n], 1)

                for b in range(UN):
                    turn(i, b + 1)
                    up(b)
                    if b >= 1:
                        down(b - 1)
                down(UN - 1)

        @block.scalar
        def _(act):
            for semaphore in (xt_in, h_in):
                act.sem_inc(semaphore, CREDIT)
            for semaphore in y_out:
                act.sem_inc(semaphore, 16 * CREDIT)
            act.wait_ge(padded, 2 + B)
            def xt_tile(i, b):
                act.wait_ge(turned[b % B], CREDIT + nth(i, b) + 1)
                act.wait_ge(h_made, CREDIT + i * UN + max(0, b - 1))
                act.activation(xt[b % 2][:], xt_ps[b % 2][:, 0:KT * P].rearrange("p (k t) -> p k t", k=KT),
                               ACT.Copy).then_inc(xt_in, 1)

            xt_tile(0, 0)
            with act.Fori(0, TURNS) as i:
                def silu_tile(b):
                    act.wait_ge(h_made, CREDIT + i * UN + (b + 1))
                    act.wait_ge(y_in, CREDIT + i * UN + max(0, b - 1))
                    act.activation(ht[b % 2][0:HALF], h_ps[b % 2][0:HALF, 0:2 * P].rearrange(
                        "p (j t) -> p j t", j=2), ACT.Silu).then_inc(h_in, 1)

                def write(b):
                    act.wait_ge(y_in, CREDIT + i * UN + (b + 1))
                    at = a["y_rows"].rearrange("(t p) n -> t p n", p=P)[i * UN + b]
                    act.dma_start(at, y_sb[b % B][:]).then_inc(y_out[b % B], 16)

                for b in range(UN):
                    xt_tile(i, b + 1)
                    silu_tile(b)
                    if b >= 2:
                        write(b - 2)
                write(UN - 2)
                write(UN - 1)

            for n in range(B):
                act.wait_ge(y_out[n], 16 * CREDIT + 16 * (TILES // B))

        @block.vector
        def _(dve):
            dve.sem_inc(y_in, CREDIT)
            for m in w2:
                dve.memset(m[:], 0.0).then_inc(padded, 1)
            for m in ht:
                dve.memset(m[:], 0.0).then_inc(padded, 1)

            with dve.Fori(0, TURNS) as i:
                for b in range(UN):
                    n = b % B
                    dve.wait_ge(y_made[n], CREDIT + nth(i, b) + 1)
                    dve.wait_ge(y_out[n], 16 * CREDIT + 16 * nth(i, b))
                    dve.tensor_copy(y_sb[n][:], y_ps[b % 2][:, 0:E]).then_inc(y_in, 1)


def combine(nc, a, keep):
    with ExitStack() as ctx:
        sb, ps, sem = scope(nc, ctx, "comb")
        x, x_t, weight, slot_i = keep["x"], keep["x_t"], keep["weight"], keep["slot_i"]
        norm = norm_parts((sb, ps, sem), keep, turn=False)
        B = 12
        got = [sb(f"got{i}", [P, E]) for i in range(B)]
        w_up = sb("w_up", [P, KT, 2 * SHARED])
        w_down = sb("w_down", [P, len(SH_TILES), E])
        sh_gate = [sb(f"sh_gate{i}", [P, CH]) for i in range(2)]
        sh_h = [sb(f"sh_h{i}", [P, len(SH_TILES), CH]) for i in range(2)]
        g_ps = [ps(f"g{i}") for i in range(2)]
        u_ps = [ps(f"u{i}") for i in range(2)]
        y_ps = [ps(f"y{i}") for i in range(2)]
        got_in = [sem(f"got_in{i}") for i in range(B)]
        w_in = sem("w_in")
        added, stored = sem("added"), sem("stored")
        gated, upped, silu, fuse, made = (sem(n) for n in ("gated", "upped", "silu", "fuse", "made"))
        ST = len(SH_TILES)
        block = ctx.enter_context(nc.Block())

        @block.sync
        def _(sp):
            sp.dma_start(w_up[:], a["w_sh_up"].rearrange("(k p) n -> p k n", p=P)).then_inc(w_in, 16)
            for m, rows in enumerate(SH_TILES):
                sp.dma_start(w_down[0:rows, m], a["w_sh_down"][m * P:m * P + rows]).then_inc(w_in, 16)
            for c in range(NCH):
                sp.wait_ge(norm["normed"], (c + 1) * TC)
                sp.dma_start(a["out"].rearrange("(t p) n -> p t n", p=P)[:, c * TC:(c + 1) * TC],
                             x[:, c * TC:(c + 1) * TC]).then_inc(stored, 16)
            sp.wait_ge(stored, 16 * NCH)

        @block.gpsimd
        def _(pool):
            for c in range(NCH):
                for n in range(c * TC * TOP, (c + 1) * TC * TOP):
                    t, k = divmod(n, TOP)
                    if n >= B:
                        pool.wait_ge(added, n - B + 1)
                    pool.indirect_dma_start(got[n % B][:], None, a["y_rows"], bass.IndirectOffsetOnAxis(
                        ap=slot_i[:, t, k:k + 1], axis=0)).then_inc(got_in[n % B], 16)
                if c >= 1:
                    norm_root(pool, norm, c - 1)
            norm_root(pool, norm, NCH - 1)

        @block.tensor
        def _(pe):
            def shared_up(c):
                for m, rows in enumerate(SH_TILES):
                    n = c * ST + m
                    for j, (bank, free, done) in enumerate(((g_ps, silu, gated), (u_ps, fuse, upped))):
                        if n >= 2:
                            pe.wait_ge(free, n - 1)
                        for k in range(KT):
                            col = j * SHARED + m * P
                            mm = pe.matmul(bank[n % 2][0:rows, :], w_up[:, k, col:col + rows],
                                           x_t[:, k, c * CH:(c + 1) * CH], start=(k == 0), stop=(k == KT - 1))
                        mm.then_inc(done, 1)

            def shared_down(c):
                for t in range(c * TC, (c + 1) * TC):
                    if t >= 2:
                        pe.wait_ge(norm["summed"], t - 1)
                    for m, rows in enumerate(SH_TILES):
                        pe.wait_ge(fuse, c * ST + m + 1)
                        mm = pe.matmul(y_ps[t % 2][:, 0:E], sh_h[c % 2][0:rows, m, t % TC * P:(t % TC + 1) * P],
                                       w_down[0:rows, m], start=(m == 0), stop=(m == ST - 1))
                    mm.then_inc(made, 1)

            pe.wait_ge(w_in, 16 * (1 + ST))
            shared_up(0)
            for c in range(1, NCH):
                shared_up(c)
                shared_down(c - 1)
            shared_down(NCH - 1)

        @block.scalar
        def _(act):
            for n in range(NCH * ST):
                rows = SH_TILES[n % ST]
                act.wait_ge(gated, n + 1)
                if n >= 2:
                    act.wait_ge(fuse, n - 1)
                act.activation(sh_gate[n % 2][0:rows], g_ps[n % 2][0:rows, :], ACT.Silu).then_inc(silu, 1)

        @block.vector
        def _(dve):
            def fuse_shared(c):
                for m, rows in enumerate(SH_TILES):
                    n = c * ST + m
                    dve.wait_ge(upped, n + 1)
                    dve.wait_ge(silu, n + 1)
                    if c >= 2:
                        dve.wait_ge(made, (c - 1) * TC)
                    dve.tensor_tensor(sh_h[c % 2][0:rows, m], u_ps[n % 2][0:rows, :], sh_gate[n % 2][0:rows],
                                      ALU.mult).then_inc(fuse, 1)

            def gather(c):
                for t in range(c * TC, (c + 1) * TC):
                    for k in range(TOP):
                        n = t * TOP + k
                        dve.wait_ge(got_in[n % B], 16 * (n // B + 1))
                        if k:
                            dve.wait_ge(added, n)
                        dve.scalar_tensor_tensor(x[:, t], got[n % B][:], weight[:, t, k:k + 1], x[:, t],
                                                 ALU.mult, ALU.add).then_inc(added, 1)
                    dve.wait_ge(added, (t + 1) * TOP)
                    dve.wait_ge(made, t + 1)
                    norm_add(dve, norm, t, y_ps[t % 2][:, 0:E])

            fuse_shared(0)
            for c in range(NCH):
                if c + 1 < NCH:
                    fuse_shared(c + 1)
                gather(c)
                norm_measure(dve, norm, c)
                if c >= 1:
                    norm_scale(dve, norm, c - 1)
            norm_scale(dve, norm, NCH - 1)


def moe(nc, a, keep):
    with ExitStack() as ctx:
        sb, ps, sem = scope(nc, ctx, "moe")
        keep = dict(keep, weight=sb("weight", [P, NT, TOP]), slot_i=sb("slot_i", [P, NT, TOP], I32),
                    tok_i=sb("tok_i", [P, TILES], I32), owner=sb("owner", [1, 2 * P], I32))
        route(nc, a, keep)
        experts(nc, a, keep)
        combine(nc, a, keep)


def program(nc, a, out, stages=9):
    with ExitStack() as ctx:
        sb, ps, sem = scope(nc, ctx, "keep")
        keep = dict(x=sb("x", [P, NT, E]), x_t=sb("x_t", [P, KT, TOK]), ident=sb("ident", [P, P]),
                    ident_bf=sb("ident_bf", [P, P], BF16), neg_half=sb("neg_half", [P, NT]))
        if stages >= 0:
            with ExitStack() as own:
                sb0 = scope(nc, own, "l0")[0]
                keep.update(v_all=sb0("v_all", [P, 2 * BATCH + 1, KTS, P]),
                            o_tok=sb0("o_tok", [P, 2 * BATCH, KTS, P]),
                            q_st=[sb0(f"q_st{i}", [P, QC, G0, CH], BF16) for i in range(2)],
                            k_st=[sb0(f"k_st{i}", [P, G0, SEQ], BF16) for i in range(2)],
                            v_st=[sb0(f"v_st{i}", [P, KTS, G0, 2 * D0]) for i in range(2)])
                project_qkv(nc, a, keep)
                attention(nc, a, keep)
                keep.update(w_up=sb0("w_up", [P, 2, KT, INTER], BF16),
                            w_down=sb0("w_down", [P, MT, E]), s_up=sb0("s_up", [P, 2, MT]),
                            s_down=sb0("s_down", [P, E]))
                project_out(nc, a, keep)
                if stages >= 2:
                    quantised_ffn(nc, a, keep)
        if stages >= 3:
            retention(nc, a, keep)
        if stages >= 4:
            moe(nc, dict(a, out=out), keep)
        else:
            store(nc, a, keep, out)


def store(nc, a, keep, out):
    with ExitStack() as ctx:
        sb, ps, sem = scope(nc, ctx, "store")
        stored = sem("stored")
        block = ctx.enter_context(nc.Block())

        @block.sync
        def _(sp):
            for c in range(NCH):
                sp.dma_start(out.rearrange("(t p) n -> p t n", p=P)[:, c * TC:(c + 1) * TC],
                             keep["x"][:, c * TC:(c + 1) * TC]).then_inc(stored, 16)
            sp.wait_ge(stored, 16 * NCH)


def lay_out(i):
    import numpy as np
    t = lambda w: np.ascontiguousarray(np.swapaxes(w, -1, -2))
    d = {}
    x = np.asarray(i["L0_attn_x"]).reshape(TOK, E)
    d["x"], d["x_t"] = x, t(x)
    w = np.asarray(i["L0_attn_w_qkv"])
    d["w_qk"], d["w_v"] = t(w[:2 * E]), t(w[2 * E:])
    d["w_out"], d["b_out"] = t(np.asarray(i["L0_attn_w_out"])), np.asarray(i["L0_attn_b_out"])
    for k in ("w_gate", "w_up", "w_down"):
        d[k] = np.asarray(i["L0_ffn_" + k]).view(np.int32)
    for k in ("s_gate", "s_up"):
        d[k] = t(np.asarray(i["L0_ffn_" + k]).reshape(MT, P))
    d["s_down"] = np.asarray(i["L0_ffn_s_down"])
    w = np.asarray(i["L1_attn_wqkv"]).reshape(H1, 3, D1, E)
    for n, k in enumerate(("w_q1", "w_k1", "w_v1")):
        d[k] = t(w[:, n].reshape(E, E))
    d["w_g1"], d["w_o1"] = t(np.asarray(i["L1_attn_wg"])), t(np.asarray(i["L1_attn_wo"]))
    d["gn_w"], d["gn_b"] = (t(np.repeat(np.asarray(i["L1_attn_gn_" + k]), D1).reshape(KT, P))
                            for k in ("weight", "bias"))
    d["tables"] = retention_tables()
    d["w_router"] = t(np.asarray(i["L1_ffn_gate_w"]))
    w1, w2 = t(np.asarray(i["L1_ffn_experts_w1"])), t(np.asarray(i["L1_ffn_experts_w2"]))
    rows = lambda w, k: np.ascontiguousarray(w.reshape(EXPERTS, k, w.shape[1] // k, w.shape[2]).transpose(
        0, 2, 1, 3).reshape(EXPERTS, w.shape[1] // k, k * w.shape[2]))
    d["w1"], d["w2"] = rows(w1, KT), rows(w2, 2)
    d["w_sh_up"], d["w_sh_down"] = t(np.asarray(i["L1_ffn_shared_gate_up"])), t(np.asarray(i["L1_ffn_shared_down"]))
    return d


def kernel(**inputs):
    import concourse.bacc as bacc
    from concourse.bass_utils import run_bass_kernel_spmd

    nc = bacc.Bacc("TRN2", target_bir_lowering=False, num_devices=1)
    arrays, a = {}, {}
    for name, v in lay_out(inputs).items():
        arrays[f"in_{name}"] = v
        a[name] = nc.dram_tensor(f"in_{name}", v.shape, mybir.dt.from_np(v.dtype), kind="ExternalInput").ap()
    scratch(nc, a)
    out = nc.dram_tensor("out_0", (TOK, E), F32, kind="ExternalOutput").ap()
    program(nc, a, out)
    r = run_bass_kernel_spmd(nc, [arrays], core_ids=[0])
    return r.results[0]["out_0"].reshape(BATCH, SEQ, E)


def scratch(nc, a):
    a["parts"] = nc.dram_tensor("parts", (GROUPS + 1, 2, PARTS, G0 * D0, SEQ), BF16, kind="Internal").ap()
    a["x_rows"] = nc.dram_tensor("x_rows", (TOK, E), F32, kind="Internal").ap()
    a["owners"] = nc.dram_tensor("owners", (2 * P,), I32, kind="Internal").ap()
    a["y_rows"] = nc.dram_tensor("y_rows", (TILES * P, E), F32, kind="Internal").ap()
```
